# Optimizing a Trainium2 kernel written in Bass

```python
import numpy as np
import jax
import jax.numpy as jnp

def _softmax(x, axis=-1):
    return jax.nn.softmax(x, axis=axis)

def _gelu(x):
    return jax.nn.gelu(x, approximate=True)

def _silu(x):
    return jax.nn.silu(x)

def _sigmoid(x):
    return jax.nn.sigmoid(x)

def _layernorm(x, axis=-1, eps=1e-05):
    m = jnp.mean(x, axis=axis, keepdims=True)
    v = jnp.var(x, axis=axis, keepdims=True)
    return (x - m) / jnp.sqrt(v + eps)

def _scatter_add(tgt, idx, src, axis=0):
    return tgt.at[idx].add(src)

def _segment_sum(src, seg, n):
    return jax.ops.segment_sum(src, seg, n)
kernel_name = 'mk_flamingo_gated_d1_seqx_r4_173103'

def setup_inputs(seed: int=0):
    np.random.seed(seed)
    _w = jnp.asarray

    def _rec_inputs():
        import jax
        import jax.numpy as jnp
        _rk = jax.random.key(seed)
        x = -0.0003929 + 0.9999 * jax.random.normal(jax.random.fold_in(_rk, 1), (32, 112, 256), jnp.float32)
        _lenS = 112 - jax.random.randint(jax.random.fold_in(_rk, 7), (32,), 0, max(1, 112 // 4) + 1, jnp.int32)
        _lenS2 = 375 - jax.random.randint(jax.random.fold_in(_rk, 8), (32,), 0, max(1, 375 // 4) + 1, jnp.int32)
        _ctx_1024P = jax.random.normal(jax.random.fold_in(_rk, 11), (32, 16, 256), jnp.float32)
        _ctx_1024c = jax.random.dirichlet(jax.random.fold_in(_rk, 511), 0.3 * jnp.ones((16,), jnp.float32), (32, 375))
        _ctx_1024t = jnp.einsum('bsk,bkd->bsd', _ctx_1024c, _ctx_1024P)
        _ctx_1024t = _ctx_1024t * jax.lax.rsqrt(jnp.mean(jnp.square(_ctx_1024t)) + 1e-12) * 0.953939
        ctx_1024 = 2.81802e-05 + 1.00001 * (_ctx_1024t + 0.3 * jax.random.normal(jax.random.fold_in(_rk, 611), (32, 375, 256), jnp.float32))
        _g = jax.random.normal(jax.random.fold_in(_rk, 9001), (2, 1), jnp.float32)
        _g = jnp.sign(_g) * jnp.maximum(jnp.abs(_g), 1.0) + (_g == 0) * 1.0
        g_xattn = _g[0]
        g_ffn = _g[1]
        return (x, ctx_1024, g_xattn, g_ffn)
    x, ctx_1024, g_xattn, g_ffn = _rec_inputs()

    def _L0_xattn_setup():
        import jax, jax.numpy as jnp
        import numpy as np
        DIM = 256
        SCALE_DIM = 4
        QK_DIM = DIM // SCALE_DIM
        B, S = (4, 1024)
        key = jax.random.key(seed)
        ks = jax.random.split(key, 8)
        std = 1.0 / np.sqrt(DIM)
        return {'q': jax.random.normal(ks[0], (B, S, DIM), jnp.float32), 'k': jax.random.normal(ks[1], (B, S, DIM), jnp.float32), 'v': jax.random.normal(ks[2], (B, S, DIM), jnp.float32), 'Wq': jax.random.normal(ks[3], (QK_DIM, DIM), jnp.float32) * std, 'bq': jnp.zeros((QK_DIM,), jnp.float32), 'Wk': jax.random.normal(ks[4], (QK_DIM, DIM), jnp.float32) * std, 'bk': jnp.zeros((QK_DIM,), jnp.float32), 'Wv': jax.random.normal(ks[5], (DIM, DIM), jnp.float32) * std, 'bv': jnp.zeros((DIM,), jnp.float32)}
    _L0_xattn_all = _L0_xattn_setup()
    _L0_xattn_in = {k: v for k, v in _L0_xattn_all.items() if k in ('Wq', 'bq', 'Wk', 'bk', 'Wv', 'bv')}
    del _L0_xattn_all

    def _L0_ffn_setup():
        import jax, jax.numpy as jnp
        import numpy as np
        TOP_K = 2
        CAPACITY = 1024
        EPS = 1e-06
        W_SCALE = 0.02

        def _rms(x, w):
            return x * jax.lax.rsqrt(jnp.mean(x * x, axis=-1, keepdims=True) + EPS) * w
        key = jax.random.key(seed)
        ks = jax.random.split(key, 8)
        B, S, H, F, E = (8, 1024, 256, 512, 8)
        F4 = F // 4
        return {'hidden_states': jax.random.normal(ks[0], (B, S, H), jnp.float32), 'Wr': jax.random.normal(ks[1], (H, E), jnp.float32) * W_SCALE, 'norm_w': jnp.ones((E, H), jnp.float32), 'Wg': jax.random.normal(ks[2], (E, H, F), jnp.float32) * W_SCALE, 'Wu': jax.random.normal(ks[3], (E, H, F), jnp.float32) * W_SCALE, 'Wd': jax.random.normal(ks[4], (E, F, H), jnp.float32) * W_SCALE, 'f_norm': jnp.ones((H,), jnp.float32), 'fWg': jax.random.normal(ks[5], (H, F4), jnp.float32) * W_SCALE, 'fWu': jax.random.normal(ks[6], (H, F4), jnp.float32) * W_SCALE, 'fWd': jax.random.normal(ks[7], (F4, H), jnp.float32) * W_SCALE}
    _L0_ffn_all = _L0_ffn_setup()
    _L0_ffn_in = {k: v for k, v in _L0_ffn_all.items() if k in ('Wr', 'norm_w', 'Wg', 'Wu', 'Wd', 'f_norm', 'fWg', 'fWu', 'fWd')}
    del _L0_ffn_all
    return {'x': x, 'ctx_1024': ctx_1024, 'g_xattn': g_xattn, 'g_ffn': g_ffn, 'L0_xattn_Wq': _L0_xattn_in['Wq'], 'L0_xattn_bq': _L0_xattn_in['bq'], 'L0_xattn_Wk': _L0_xattn_in['Wk'], 'L0_xattn_bk': _L0_xattn_in['bk'], 'L0_xattn_Wv': _L0_xattn_in['Wv'], 'L0_xattn_bv': _L0_xattn_in['bv'], 'L0_ffn_Wr': _L0_ffn_in['Wr'], 'L0_ffn_norm_w': _L0_ffn_in['norm_w'], 'L0_ffn_Wg': _L0_ffn_in['Wg'], 'L0_ffn_Wu': _L0_ffn_in['Wu'], 'L0_ffn_Wd': _L0_ffn_in['Wd'], 'L0_ffn_f_norm': _L0_ffn_in['f_norm'], 'L0_ffn_fWg': _L0_ffn_in['fWg'], 'L0_ffn_fWu': _L0_ffn_in['fWu'], 'L0_ffn_fWd': _L0_ffn_in['fWd']}

def reference(x, ctx_1024, g_xattn, g_ffn, L0_xattn_Wq, L0_xattn_bq, L0_xattn_Wk, L0_xattn_bk, L0_xattn_Wv, L0_xattn_bv, L0_ffn_Wr, L0_ffn_norm_w, L0_ffn_Wg, L0_ffn_Wu, L0_ffn_Wd, L0_ffn_f_norm, L0_ffn_fWg, L0_ffn_fWu, L0_ffn_fWd):
    import jax
    import jax.numpy as jnp

    def _L0_xattn_ref(q, k, v, Wq, bq, Wk, bk, Wv, bv):
        import jax, jax.numpy as jnp
        import numpy as np
        DIM = 256
        SCALE_DIM = 4
        QK_DIM = DIM // SCALE_DIM
        B, S = (4, 1024)
        scale = jnp.asarray(np.sqrt(QK_DIM), q.dtype)
        qp = jnp.einsum('bsd,ed->bse', q, Wq) + bq
        kp = jnp.einsum('bsd,ed->bse', k, Wk) + bk
        vp = jnp.einsum('bsd,ed->bse', v, Wv) + bv
        z = jnp.einsum('bqe,bke->bqk', qp, kp)
        z = jax.nn.sigmoid(z / scale)
        return jnp.einsum('bqk,bkd->bqd', z, vp)

    def _L0_ffn_ref(hidden_states, Wr, norm_w, Wg, Wu, Wd, f_norm, fWg, fWu, fWd):
        import jax, jax.numpy as jnp
        import numpy as np
        TOP_K = 2
        CAPACITY = 1024
        EPS = 1e-06
        W_SCALE = 0.02

        def _rms(x, w):
            return x * jax.lax.rsqrt(jnp.mean(x * x, axis=-1, keepdims=True) + EPS) * w
        B, S, H = hidden_states.shape
        E = Wr.shape[1]
        N = B * S
        x = hidden_states.reshape(N, H)
        probs = jax.nn.softmax(x @ Wr, axis=-1)
        w_topk, e_topk = jax.lax.top_k(probs, TOP_K)
        e_flat = e_topk.reshape(-1)
        oh = jax.nn.one_hot(e_flat, E, dtype=jnp.int32)
        pos = jnp.take_along_axis(jnp.cumsum(oh, axis=0) - 1, e_flat[:, None], axis=1)[:, 0]
        keep = pos < CAPACITY
        x_rep = jnp.repeat(x, TOP_K, axis=0)
        buf = jnp.zeros((E, CAPACITY, H), x.dtype).at[e_flat, pos].set(x_rep, mode='drop')
        h = _rms(buf, norm_w[:, None, :])
        gate = jax.nn.gelu(jnp.einsum('ech,ehf->ecf', h, Wg), approximate=False)
        up = jnp.einsum('ech,ehf->ecf', h, Wu)
        buf_out = jnp.einsum('ecf,efh->ech', gate * up, Wd) + buf
        exp_out = buf_out[e_flat, jnp.minimum(pos, CAPACITY - 1)]
        contrib = w_topk.reshape(-1)[:, None] * exp_out * keep[:, None].astype(x.dtype)
        combined = x + contrib.reshape(N, TOP_K, H).sum(axis=1)
        overflow = (~keep).reshape(N, TOP_K).any(axis=1)
        fh = _rms(x, f_norm)
        fout = jax.nn.gelu(fh @ fWg, approximate=False) * (fh @ fWu) @ fWd + x
        out = jnp.where(overflow[:, None], fout, combined)
        return out.reshape(B, S, H)
    x = x + jnp.tanh(g_xattn[0]) * _L0_xattn_ref(_layernorm(x, axis=-1), ctx_1024, ctx_1024, L0_xattn_Wq, L0_xattn_bq, L0_xattn_Wk, L0_xattn_bk, L0_xattn_Wv, L0_xattn_bv)
    x = x + jnp.tanh(g_ffn[0]) * _L0_ffn_ref(_layernorm(x, axis=-1), L0_ffn_Wr, L0_ffn_norm_w, L0_ffn_Wg, L0_ffn_Wu, L0_ffn_Wd, L0_ffn_f_norm, L0_ffn_fWg, L0_ffn_fWu, L0_ffn_fWd)
    return x

_drawn_inputs = setup_inputs


def setup_inputs(seed=0):
    import zlib

    import numpy as np

    out = dict(_drawn_inputs(seed))
    spreads = {'L0_xattn_bq': (0.0, 0.271),
     'L0_xattn_bk': (0.0, 0.1),
     'L0_xattn_bv': (0.0, 0.1),
     'L0_ffn_norm_w': (1.0, 0.6),
     'L0_ffn_f_norm': (1.0, 0.6)}
    factors = {'L0_ffn_Wr': 8.0,
     'L0_ffn_Wg': 8.0,
     'L0_ffn_Wu': 8.0,
     'L0_ffn_Wd': 8.0,
     'L0_ffn_fWg': 8.0,
     'L0_ffn_fWu': 8.0,
     'L0_ffn_fWd': 8.0}
    for name, (base, spread) in spreads.items():
        noise = np.random.default_rng([zlib.crc32(name.encode()), seed]).standard_normal(out[name].shape)
        drawn = base * np.exp(spread * noise) if base else spread * noise
        out[name] = jnp.asarray(drawn.astype(out[name].dtype))
    for name, factor in factors.items():
        out[name] = (out[name] * factor).astype(out[name].dtype)
    return out
```

```python
import numpy as np
import concourse.bass as bass
from concourse import mybir
from contextlib import ExitStack

F32 = mybir.dt.float32
F32R = mybir.dt.float32r
I32 = mybir.dt.int32
U32 = mybir.dt.uint32
ALU = mybir.AluOpType
ACT = mybir.ActivationFunctionType
AX = mybir.AxisListType

B, S, H, C = 32, 112, 256, 375
KC = C // 3
QK = 64
E, F, FB = 8, 512, 128
E2 = E + 2
CAP = 1024
N = B * S
G = 4
UNIT = 256
COLS = E * CAP // 128
FCOLS = 32
TABLE = COLS + FCOLS
UNITS = 48
PAY = 272
W_FB, W_INV, W_NONE = H + E, H + E + 1, H + E + 2
DUMMY = UNIT
LN_EPS, RMS_EPS = 1e-5, 1e-6


class Chain:

    def __init__(self, engine, sem):
        self.engine, self.sem, self.n = engine, sem, 0

    def put(self, ins):
        ins.then_inc(self.sem, 1)
        self.n += 1

    def link(self, ins):
        self.put(ins)
        self.engine.wait_ge(self.sem, self.n)

    def wait(self):
        self.engine.wait_ge(self.sem, self.n)

    def restart(self):
        if self.n:
            self.engine.wait_ge(self.sem, self.n)
            self.engine.sem_clear(self.sem)
            self.n = 0


def settle(engine, sem):
    engine.sem_inc(sem, 1)


class Counts:

    def __init__(self, engine, j):
        self.engine, self.j, self.kept = engine, j, {}

    def __call__(self, a, c):
        if isinstance(self.j, int):
            return a * self.j + c
        if (a, c) not in self.kept:
            self.kept[a, c] = self.engine.snap(self.j * a + c)
        return self.kept[a, c]

    def wait(self, sem, a, c):
        v = self(a, c)
        if not isinstance(v, int) or v > 0:
            self.engine.wait_ge(sem, v)


def build(nc, x, ctx_rows, g2, wqT, bq, wkT, bk, wvT, bv, wr, norms, wg, wu, wd, fwg, fwu, fwd, out):
    stack = ExitStack()
    with stack:
        def sb(name, shape, dt=F32):
            return stack.enter_context(nc.sbuf_tensor(name, shape, dt))

        def sem(name):
            return stack.enter_context(nc.semaphore(name))

        payload = nc.dram_tensor("payload", [N, PAY], F32).ap()

        ident = sb("ident", [128, 128])
        before = sb("before", [S, S])
        ones = sb("ones", [128, 128])
        before_r = sb("before_r", [S, S], F32R)
        ones_r = sb("ones_r", [S, 128], F32R)
        iota_i = sb("iota_i", [128, 128], I32)
        iota_f = sb("iota_f", [128, 128])
        rev8 = sb("rev8", [S, E])
        ids = sb("ids", [S, G])
        ids_i = sb("ids_i", [S, G], I32)
        dummy_i = sb("dummy_i", [128, 2], I32)
        dummy_f = sb("dummy_f", [128, 2])
        zeros = sb("zeros", [128, 2 * H])
        exp_base = sb("exp_base", [S, G * E])
        exp3 = sb("exp3", [S, 3])
        gates = sb("gates", [128, 2])
        tg = sb("tg", [128, 2])
        wq_sb = sb("wq_sb", [128, 2, QK])
        wk_sb = sb("wk_sb", [128, 2, QK])
        wv_sb = sb("wv_sb", [128, 2, H])
        wr_sb = sb("wr_sb", [128, 2, E])
        bq_sb = sb("bq_sb", [QK, 1])
        bk_sb = sb("bk_sb", [QK, 1])
        bv_sb = sb("bv_sb", [S, H])
        norms_sb = sb("norms_sb", [128, E + 1, 2])

        x_sb = sb("x_sb", [S, 4, H])
        ctx_sb = sb("ctx_sb", [KC, 4, 3, H])
        stat1 = sb("stat1", [S, 2, 6])
        mv1 = sb("mv1", [S, 2, 2])
        arg1 = sb("arg1", [S, 2, 1])
        rs1 = sb("rs1", [S, 2, 1])
        y_sb = sb("y_sb", [S, 2, H])
        yT = sb("yT", [128, 2, S])
        ctxT = sb("ctxT", [128, 2, C])
        kpT = sb("kpT", [QK, C])
        qpT = sb("qpT", [QK, S])
        z_sb = sb("z_sb", [KC, 2, 3, S])
        avT = sb("avT", [128, 2, S])
        xb = sb("xb", [S, 2, H])
        x1 = sb("x1", [S, 2, H])
        stat2 = sb("stat2", [S, 2, 6])
        mv2 = sb("mv2", [S, 2, 2])
        arg3 = sb("arg3", [S, 2, 3])
        rs3 = sb("rs3", [S, 2, 3])
        ab = sb("ab", [S, 2, 3])
        h_sb = sb("h_sb", [S, 2, H])
        base = sb("base", [S, 2, H])
        hT = sb("hT", [128, 2, S])
        logit = sb("logit", [S, G, E])
        inv_g = sb("inv_g", [S, G])
        m12 = sb("m12", [S, 2, G])
        eq = sb("eq", [S, G, E])
        rest = sb("rest", [S, G, E])
        mi3 = sb("mi3", [S, G, 3])
        oh = sb("oh", [S, G, 2, E])
        cnt = sb("cnt", [S, G, E], F32R)
        cnt2 = sb("cnt2", [S, G, E2], F32R)
        carry = sb("carry", [S, E2], F32R)
        carry2 = sb("carry2", [S, E2], F32R)
        csum = sb("csum", [S, E2])
        expo = sb("expo", [S, G * E])
        ex = sb("ex", [S, G * E])
        den = sb("den", [S, 2, G])
        wnum = sb("wnum", [S, G, E])
        extra = sb("extra", [S, G, PAY - H])
        pm = sb("pm", [S, G, 2, E])
        pos = sb("pos", [S, G, 2])
        drop = sb("drop", [S, G, 2])
        ovf = sb("ovf", [S, G])
        keep = sb("keep", [S, G])
        cpos = sb("cpos", [S, G, 3])
        pen = sb("pen", [S, G, 3])
        slot_i = sb("slot_i", [S, G * 3], I32)
        lc_i = sb("lc_i", [S, 2, G * 3], I32)
        lc = sb("lc", [S, 2, G * 3])
        hot_lo = sb("hot_lo", [S, G * 3, 128], F32R)
        hot_col = sb("hot_col", [S, G * 3, TABLE], F32R)
        table = sb("table", [128, TABLE])
        gidx_f = sb("gidx_f", [128, TABLE])
        gidx = sb("gidx", [128, TABLE], I32)
        empty = sb("empty", [128, TABLE])
        sidx = sb("sidx", [128, TABLE], I32)
        tot_f = sb("tot_f", [1, E + 1])
        tot_i = sb("tot_i", [1, E + 1], I32)
        nun = sb("nun", [1, E + 1])
        cum = sb("cum", [1, E + 2])
        cum_i = sb("cum_i", [1, E + 2], I32)
        step8 = sb("step8", [1, E])
        ucol3 = sb("ucol3", [1, UNITS, E])
        ucol_f = sb("ucol_f", [1, UNITS])
        ucol = sb("ucol", [1, UNITS], I32)
        wg_sb = [sb(f"wg_sb{q}", [128, 2, F]) for q in range(2)]
        wu_sb = [sb(f"wu_sb{q}", [128, 2, F]) for q in range(2)]
        wd_sb = [sb(f"wd_sb{q}", [128, 4, H]) for q in range(2)]
        fwg_sb = sb("fwg_sb", [128, 2, FB])
        fwu_sb = sb("fwu_sb", [128, 2, FB])
        fwd_sb = sb("fwd_sb", [128, 1, H])
        gidx_now = sb("gidx_now", [128, 2], I32)
        sidx_now = sb("sidx_now", [128, 2], I32)
        hg = [sb(f"hg{s}", [128, PAY]) for s in range(2)]
        w_now = sb("w_now", [128, 2])
        wi_now = sb("wi_now", [128, 2])
        norm_now = sb("norm_now", [128, 2])
        hw = sb("hw", [128, 2, H])
        hgT = sb("hgT", [128, 2, UNIT])
        gel = sb("gel", [128, 2, UNIT])
        act = sb("act", [128, 4, UNIT])
        yo = sb("yo", [128, 2, H])

        bank = [stack.enter_context(nc.psum_tensor(f"bank{i}", [128, 512], F32)) for i in range(8)]
        ps_c0, ps_c1 = bank[0], bank[1]
        ps_q, ps_k, ps_s, ps_v, ps_o, ps_r = bank[2:8]
        r_logit = ps_r[0:S, 0:E]
        r_pos = ps_r[0:S, 32:32 + G * E].rearrange("p (g e) -> p g e", e=E)
        r_pos2 = ps_r[0:S, 64:64 + G * E2].rearrange("p (g e) -> p g e", e=E2)
        r_tab = ps_r[:, 128:128 + TABLE]
        r_tot = ps_r[:, 256:256 + E + 2]

        names = ("const_in wts_in w_aff c_gp c_dve c_tanh dve_own act_own pool_own "
                 "st1 rs1_ok y_ok yT_ps c0_ps c1_ps yT_ok c0_ok c1_ok kp_ps qp_ps kp_ok qp_ok s_ps z_ok "
                 "av_ps av_ok o_ps x1_ok st2 rs3_ok h_ok base_ok hT_ps hT_ok lg_ps lg_ok "
                 "top_ok ex_ok pos_ps pos_rd cnt2_ok pos2_ps pos2_rd wd_ok hot_ok tab_ps tab_ok ext_out "
                 "tot_ps plan_ok fill_out w_in0 w_in1 fw_in exp_done gT_ps gT_ok wi_ok hw_ok yo_ok yo_free "
                 "dn_ps settled").split()
        s = {n: sem(n) for n in names}
        x_in = [sem(f"x_in{i}") for i in range(4)]
        ctx_in = [sem(f"ctx_in{i}") for i in range(4)]
        h_out = [sem(f"h_out{i}") for i in range(2)]
        base_out = [sem(f"base_out{i}") for i in range(2)]
        hg_in = [sem(f"hg_in{i}") for i in range(2)]
        added = [sem(f"added{i}") for i in range(2)]
        gate_ps = [sem(f"gate_ps{i}") for i in range(4)]
        up_ps = [sem(f"up_ps{i}") for i in range(4)]
        gel_ok = [sem(f"gel_ok{i}") for i in range(4)]
        act_ok = [sem(f"act_ok{i}") for i in range(4)]

        LAST = B // G - 1
        N_CONST = 9

        def groups(engine, body, first=0, loop=(2, 7), last=LAST + 2):
            for j in range(first, loop[0]):
                body(j)
            with engine.Fori(loop[0], loop[1]) as j:
                body(j)
            for j in range(loop[1], last):
                body(j)

        def there(j, k, off):
            return not isinstance(j, int) or 0 <= G * j + k + off < B

        def group_there(j, off):
            return not isinstance(j, int) or 0 <= j + off <= LAST

        block = stack.enter_context(nc.Block())

        @block.sync
        def _(sp):
            with nc.allow_non_contiguous_dma(reason="small constants"):
                sp.dma_start(gates[:], g2.rearrange("(o a) -> o a", o=1).to_broadcast([128, 2])).then_inc(s["const_in"], 16)
                sp.dma_start(bq_sb[:], bq.rearrange("(p o) -> p o", o=1)).then_inc(s["const_in"], 16)
                sp.dma_start(bk_sb[:], bk.rearrange("(p o) -> p o", o=1)).then_inc(s["const_in"], 16)
                sp.dma_start(bv_sb[:], bv.rearrange("(o a) -> o a", o=1).to_broadcast([S, H])).then_inc(s["const_in"], 16)
                sp.dma_start(norms_sb[:], norms).then_inc(s["const_in"], 16)
            sp.dma_start(wv_sb[:], wvT.rearrange("(k p) d -> p k d", p=128)).then_inc(s["const_in"], 16)

            def load(sp_row, ctx_row, slot):
                sp.dma_start(x_sb[:, slot, :], x[bass.ds(sp_row, S), :]).then_inc(x_in[slot], 16)
                sp.dma_start(ctx_sb[0:S, slot],
                             ctx_rows[bass.ds(ctx_row, 3 * S), :].rearrange("(p c) d -> p c d", c=3)).then_inc(ctx_in[slot], 16)
                sp.dma_start(ctx_sb[S:KC, slot],
                             ctx_rows[bass.ds(ctx_row + 3 * S, C - 3 * S), :].rearrange("(p c) d -> p c d", c=3)).then_inc(ctx_in[slot], 16)

            load(0, 0, 0)
            sp.dma_start(wq_sb[:], wqT.rearrange("(k p) d -> p k d", p=128)).then_inc(s["const_in"], 16)
            sp.dma_start(wk_sb[:], wkT.rearrange("(k p) d -> p k d", p=128)).then_inc(s["const_in"], 16)
            sp.dma_start(wr_sb[:], wr.rearrange("(k p) d -> p k d", p=128)).then_inc(s["const_in"], 16)
            load(S, C, 1)
            load(2 * S, 2 * C, 2)
            sp.wait_ge(s["c_gp"], 1)
            sp.dma_start(out[N:N + DUMMY, :].rearrange("(p c) d -> p (c d)", c=2), zeros[:]).then_inc(s["fill_out"], 16)

            def expert_weights(e, q, w_in):
                sp.dma_start(wg_sb[q][:], wg[e].rearrange("(k p) f -> p k f", p=128)).then_inc(w_in, 16)
                sp.dma_start(wu_sb[q][:], wu[e].rearrange("(k p) f -> p k f", p=128)).then_inc(w_in, 16)
                sp.dma_start(wd_sb[q][:], wd[e].rearrange("(k p) d -> p k d", p=128)).then_inc(w_in, 16)

            def steps(j):
                n = Counts(sp, j)
                for k in range(4):
                    if there(j, k, 3):
                        n.wait(s["x1_ok"], 4, k)
                        load(G * S * j + (k + 3) * S, G * C * j + (k + 3) * C, (k + 3) % 4)
                    if there(j, k, -1):
                        row = G * S * j + (k - 1) * S
                        p = (k - 1) % 2
                        n.wait(s["h_ok"], 4, k)
                        sp.dma_start(payload[bass.ds(row, S), 0:H], h_sb[:, p, :]).then_inc(h_out[p], 16)
                        n.wait(s["base_ok"], 4, k)
                        sp.dma_start(out[bass.ds(row, S), :], base[:, p, :]).then_inc(base_out[p], 16)
                    if k == 3 and group_there(j, -1):
                        n.wait(s["wd_ok"], 1, 0)
                        with nc.allow_non_contiguous_dma(reason="64 B of weights per token"):
                            sp.dma_start(payload[bass.ds(G * S * (j - 1), G * S), H:PAY].rearrange("(g p) c -> p g c", g=G),
                                         extra[:]).then_inc(s["ext_out"], 16)

            for j in range(0, 2):
                steps(j)
            expert_weights(0, 0, s["w_in0"])
            expert_weights(1, 1, s["w_in1"])
            sp.dma_start(fwg_sb[:], fwg.rearrange("(k p) f -> p k f", p=128)).then_inc(s["fw_in"], 16)
            sp.dma_start(fwu_sb[:], fwu.rearrange("(k p) f -> p k f", p=128)).then_inc(s["fw_in"], 16)
            sp.dma_start(fwd_sb[:], fwd.rearrange("(k p) d -> p k d", p=128)).then_inc(s["fw_in"], 16)
            groups(sp, steps, first=2)
            with sp.Fori(1, E // 2) as i:
                for q in range(2):
                    sp.wait_ge(s["exp_done"], sp.snap(2 * i + (q - 1)))
                    for buf, src, kk in ((wg_sb, wg, 2), (wu_sb, wu, 2), (wd_sb, wd, 4)):
                        sp.dma_start(buf[q][:], src[bass.ds(2 * i + q, 1)].rearrange("o (k p) f -> p (o k) f", p=128)).then_inc(s[f"w_in{q}"], 16)
            for p in range(2):
                sp.wait_ge(base_out[p], 16 * B // 2)

        @block.gpsimd
        def _(pool):
            own = Chain(pool, s["pool_own"])
            gp = nc.gpsimd
            own.put(gp.memset(ones[:], 1.0))
            own.put(gp.iota(iota_i[:], [[1, 128]], 0, 0))
            own.put(gp.iota(ids_i[:], [[S, G]], 1, 1))
            own.put(gp.iota(dummy_i[:], [[128, 2]], N + 1, 1))
            own.put(gp.memset(exp_base[:], float(np.e)))
            own.put(gp.memset(exp3[:, 0:2], -0.5))
            own.put(gp.memset(exp3[:, 2:3], 0.5))
            own.put(gp.memset(mi3[:], 0.0))
            own.put(gp.memset(extra[:], 0.0))
            own.put(gp.memset(table[:], 0.0))
            own.put(gp.memset(cnt2[:].bitcast(F32), 0.0))
            own.put(gp.memset(carry[:].bitcast(F32), 0.0))
            own.put(gp.memset(carry2[:].bitcast(F32), 0.0))
            own.link(gp.memset(zeros[:], 0.0))
            own.put(gp.affine_select(out=ident[:], in_=ones[:], compare_op=ALU.is_equal, fill=0.0, base=0,
                                     pattern=[[-1, 128]], channel_multiplier=1))
            own.link(gp.affine_select(out=before[:], in_=ones[0:S, 0:S], compare_op=ALU.is_gt, fill=0.0, base=0,
                                      pattern=[[1, S]], channel_multiplier=-1))
            pool.sem_inc(s["c_gp"], 1)
            pool.sem_inc(s["yo_free"], 1)
            pool.wait_ge(s["c_tanh"], 3)

            def steps(j, only=range(4)):
                n = Counts(pool, j)
                for k in only:
                    if there(j, k, -1):
                        p = (k - 1) % 2
                        n.wait(s["st2"], 4, k)
                        settle(pool, s["settled"])
                        own.put(gp.tensor_scalar(arg3[:, p, 0:1], mv2[:, p, 1:2], 1.0 + RMS_EPS, RMS_EPS * LN_EPS, ALU.mult, ALU.add))
                        own.put(gp.tensor_scalar(arg3[:, p, 2:3], mv2[:, p, 1:2], 1.0 + RMS_EPS, RMS_EPS * LN_EPS, ALU.mult, ALU.add))
                        own.link(gp.tensor_scalar(arg3[:, p, 1:2], mv2[:, p, 1:2], 1.0, LN_EPS, ALU.mult, ALU.add))
                        gp.tensor_tensor(rs3[:, p, :], arg3[:, p, :], exp3[:], ALU.pow).then_inc(s["rs3_ok"], 1)
                    if there(j, k, 2):
                        p = k % 2
                        n.wait(s["st1"], 4, k + 3)
                        settle(pool, s["settled"])
                        own.link(gp.tensor_scalar(arg1[:, p, :], mv1[:, p, 1:2], 1.0, LN_EPS, ALU.mult, ALU.add))
                        gp.tensor_tensor(rs1[:, p, :], arg1[:, p, :], exp3[:, 0:1], ALU.pow).then_inc(s["rs1_ok"], 1)
                    if there(j, k, -1):
                        p = (k - 1) % 2
                        n.wait(s["rs3_ok"], 4, k)
                        own.put(gp.tensor_tensor(inv_g[:, (k - 1) % 4:(k - 1) % 4 + 1], rs3[:, p, 1:2], rs3[:, p, 2:3], ALU.mult))
                        own.put(gp.tensor_scalar(ab[:, p, 0:1], rs3[:, p, 1:2], tg[0:S, 1:2], 1.0, ALU.mult, ALU.add))
                        own.link(gp.tensor_tensor(ab[:, p, 2:3], mv2[:, p, 0:1], rs3[:, p, 1:2], ALU.mult))
                        own.link(gp.tensor_scalar(ab[:, p, 1:2], ab[:, p, 2:3], tg[0:S, 1:2], -1.0, ALU.mult, ALU.mult))
                        n.wait(base_out[p], 32, 16 * ((k - 1) // 2))
                        settle(pool, s["settled"])
                        gp.tensor_scalar(base[:, p, :], x1[:, p, :], ab[:, p, 0:1], ab[:, p, 1:2], ALU.mult, ALU.add).then_inc(s["base_ok"], 1)
                    if k == 0 and group_there(j, -1):
                        n.wait(s["top_ok"], 1, 0)
                        gp.tensor_tensor(ex[:], exp_base[:], expo[:], ALU.pow).then_inc(s["ex_ok"], 1)
                own.restart()

            for t in range(2):
                pool.wait_ge(s["st1"], t + 1)
                own.link(gp.tensor_scalar(arg1[:, t, :], mv1[:, t, 1:2], 1.0, LN_EPS, ALU.mult, ALU.add))
                gp.tensor_tensor(rs1[:, t, :], arg1[:, t, :], exp3[:, 0:1], ALU.pow).then_inc(s["rs1_ok"], 1)
            own.restart()
            groups(pool, steps)

            pool.wait_ge(s["plan_ok"], 1)
            pool.wait_ge(s["ext_out"], 16 * (B // G))
            pool.wait_ge(s["fill_out"], 16)
            for p in range(2):
                pool.wait_ge(h_out[p], 16 * B // 2)
                pool.wait_ge(base_out[p], 16 * B // 2)

            def gather(col):
                own.link(gp.tensor_copy(gidx_now[:], gidx[:, bass.ds(col, 2)]))
                for i in range(2):
                    gp.indirect_dma_start(out=hg[i][:], out_offset=None, in_=payload,
                                          in_offset=bass.IndirectOffsetOnAxis(ap=gidx_now[:, i:i + 1], axis=0)).then_inc(hg_in[i], 16)

            n_units = pool.value_load(cum_i[0:1, E + 1:E + 2], min_val=E + 1, max_val=UNITS - 1)
            col0 = pool.value_load(ucol[0:1, 0:1], min_val=0, max_val=TABLE - 2)
            gather(col0)
            own.restart()
            with pool.Fori(0, n_units) as g:
                col = pool.value_load(ucol[0:1, bass.ds(g, 1)], min_val=0, max_val=TABLE - 2)
                own.link(gp.tensor_copy(sidx_now[:], sidx[:, bass.ds(col, 2)]))
                nxt = pool.value_load(ucol[0:1, bass.ds(g + 1, 1)], min_val=0, max_val=TABLE - 2)
                g1 = pool.snap(g + 1)
                g16 = pool.snap(g * 16 + 16)
                for i in range(2):
                    pool.wait_ge(hg_in[i], g16)
                pool.wait_ge(s["gT_ps"], g1)
                pool.wait_ge(s["hw_ok"], g1)
                gather(nxt)
                pool.wait_ge(s["yo_ok"], pool.snap(g + 2))
                settle(pool, s["settled"])
                for i in range(2):
                    gp.indirect_dma_start(out=out, out_offset=bass.IndirectOffsetOnAxis(ap=sidx_now[:, i:i + 1], axis=0),
                                          in_=yo[:, i, :], in_offset=None, compute_op=ALU.add).then_inc(added[i], 16)
                for i in range(2):
                    pool.wait_ge(added[i], g16)
                pool.sem_inc(s["yo_free"], 1)
                own.restart()
            for i in range(2):
                pool.wait_ge(hg_in[i], pool.snap(n_units * 16 + 16))

        @block.scalar
        def _(act_e):
            sc = nc.scalar
            act_e.wait_ge(s["const_in"], 16 * N_CONST)
            sc.activation(tg[:], gates[:], ACT.Tanh).then_inc(s["c_tanh"], 1)
            act_e.wait_ge(s["c_tanh"], 1)
            sc.activation(wv_sb[:], wv_sb[:], ACT.Copy, scale=tg[:, 0:1]).then_inc(s["c_tanh"], 1)
            sc.activation(bv_sb[:], bv_sb[:], ACT.Copy, scale=tg[0:S, 0:1]).then_inc(s["c_tanh"], 1)

            def head(n, k, off):
                c = k + off + 1
                n.wait(s["yT_ps"], 4, c)
                sc.activation(yT[:], ps_q[:, 0:2 * S].rearrange("p (k q) -> p k q", k=2), ACT.Copy).then_inc(s["yT_ok"], 1)
                n.wait(s["c1_ps"], 4, c)
                sc.activation(ctxT[:, 1, :], ps_c1[:, 0:C], ACT.Copy).then_inc(s["c1_ok"], 1)

            def proj(n, k, off):
                c = k + off + 1
                n.wait(s["kp_ps"], 4, c)
                sc.activation(kpT[:], ps_k[0:QK, 0:C], ACT.Identity, bias=bk_sb[:]).then_inc(s["kp_ok"], 1)
                n.wait(s["qp_ps"], 4, c)
                sc.activation(qpT[:], ps_q[0:QK, 2 * S:3 * S], ACT.Identity, bias=bq_sb[:]).then_inc(s["qp_ok"], 1)

            def steps(j, only=range(4)):
                n = Counts(act_e, j)
                for k in only:
                    if there(j, k, 0):
                        n.wait(s["s_ps"], 4, k + 1)
                        sc.activation(z_sb[:, k % 2], ps_s[0:KC, 0:3 * S].rearrange("p (c q) -> p c q", c=3),
                                      ACT.Sigmoid, scale=1.0 / float(np.sqrt(QK))).then_inc(s["z_ok"], 1)
                    if there(j, k, 1):
                        head(n, k, 1)
                    if there(j, k, 0):
                        n.wait(s["av_ps"], 4, k + 1)
                        sc.activation(avT[:], ps_v[:, 0:2 * S].rearrange("p (k q) -> p k q", k=2), ACT.Copy).then_inc(s["av_ok"], 1)
                    if there(j, k, 1):
                        proj(n, k, 1)
                    if there(j, k, -1):
                        n.wait(s["hT_ps"], 4, k)
                        sc.activation(hT[:], ps_v[:, 2 * S:4 * S].rearrange("p (k q) -> p k q", k=2), ACT.Copy).then_inc(s["hT_ok"], 1)

            n = Counts(act_e, 0)
            head(n, -1, 1)
            proj(n, -1, 1)
            groups(act_e, steps)

            act_e.wait_ge(s["plan_ok"], 1)

            def unit(g, ft):
                g1 = act_e.snap(g + 1)
                act_e.wait_ge(s["wi_ok"], g1)
                act_e.wait_ge(s["yo_ok"], g1)
                sc.activation(hw[:, 0, :], hg[0][:, 0:H], ACT.Copy, scale=wi_now[:, 0:1])
                sc.activation(hw[:, 1, :], hg[1][:, 0:H], ACT.Copy, scale=wi_now[:, 1:2]).then_inc(s["hw_ok"], 1)
                for f in range(ft):
                    act_e.wait_ge(gate_ps[f], g1)
                    if f >= 2:
                        act_e.wait_ge(act_ok[f - 2], g1)
                    sc.activation(gel[:, f % 2, :], bank[1 + f % 2][:, 0:UNIT], ACT.Gelu).then_inc(gel_ok[f], 1)

            n_exp = act_e.value_load(cum_i[0:1, E:E + 1], min_val=E, max_val=UNITS - 2)
            with act_e.Fori(0, n_exp) as g:
                unit(g, 4)
            n_all = act_e.value_load(cum_i[0:1, E + 1:E + 2], min_val=E + 1, max_val=UNITS - 1)
            with act_e.Fori(n_exp, n_all) as g:
                unit(g, 1)

        @block.vector
        def _(dve):
            own = Chain(dve, s["dve_own"])
            v = nc.vector
            dve.sem_inc(s["yo_ok"], 1)
            dve.wait_ge(s["c_gp"], 1)
            own.put(v.tensor_copy(before_r[:], before[:]))
            own.put(v.tensor_copy(ones_r[:], ones[0:S, :]))
            own.put(v.tensor_copy(ids[:], ids_i[:]))
            own.put(v.tensor_copy(dummy_f[:], dummy_i[:]))
            own.link(v.tensor_copy(iota_f[:], iota_i[:]))
            own.put(v.tensor_scalar(rev8[:], iota_f[0:S, 0:E], -1.0, float(E), ALU.mult, ALU.add))
            dve.wait_ge(s["c_tanh"], 3)
            own.put(v.tensor_copy(extra[:, :, E:E + 1], tg[0:S, 1:2].unsqueeze(1).to_broadcast([S, G, 1])))
            own.wait()
            dve.sem_inc(s["c_dve"], 1)

            def stats1(n, k, off):
                slot, p = (k + off) % 4, (k + off) % 2
                n.wait(x_in[slot], 16, 16 * ((k + off) // 4 + 1))
                own.link(v.bn_stats(stat1[:, p, :], x_sb[:, slot, :]))
                v.bn_aggr(mv1[:, p, :], stat1[:, p, :]).then_inc(s["st1"], 1)

            def normal1(n, k, off):
                slot, p = (k + off) % 4, (k + off) % 2
                n.wait(s["rs1_ok"], 4, k + off + 1)
                v.tensor_scalar(y_sb[:, p, :], x_sb[:, slot, :], mv1[:, p, 0:1], rs1[:, p, :],
                                ALU.subtract, ALU.mult).then_inc(s["y_ok"], 1)

            def ctx_half(n, k, off):
                n.wait(s["c0_ps"], 4, k + off + 1)
                v.tensor_copy(ctxT[:, 0, :], ps_c0[:, 0:C]).then_inc(s["c0_ok"], 1)

            def top2():
                rev = rev8[:].unsqueeze(1).to_broadcast([S, G, E])
                own.link(v.tensor_reduce(out=m12[:, 0, :], in_=logit[:], axis=AX.X, op=ALU.max))
                src = logit
                for i in range(2):
                    mx = m12[:, i, :].unsqueeze(2).to_broadcast([S, G, E])
                    own.link(v.tensor_tensor(eq[:], src[:], mx, ALU.is_equal))
                    own.link(v.tensor_tensor(eq[:], eq[:], rev, ALU.mult))
                    own.link(v.tensor_reduce(out=mi3[:, :, i], in_=eq[:], axis=AX.X, op=ALU.max))
                    own.link(v.tensor_tensor(oh[:, :, i, :], rev, mi3[:, :, i:i + 1].to_broadcast([S, G, E]), ALU.is_equal))
                    if i == 0:
                        own.link(v.scalar_tensor_tensor(rest[:], oh[:, :, 0, :], -1e30, logit[:], ALU.mult, ALU.add))
                        own.link(v.tensor_reduce(out=m12[:, 1, :], in_=rest[:], axis=AX.X, op=ALU.max))
                        src = rest
                own.link(v.tensor_tensor(rest[:], logit[:], m12[:, 0, :].unsqueeze(2).to_broadcast([S, G, E]), ALU.subtract))
                own.put(v.tensor_tensor(expo[:].rearrange("p (g e) -> p g e", e=E), rest[:],
                                        inv_g[:].unsqueeze(2).to_broadcast([S, G, E]), ALU.mult))
                own.link(v.tensor_copy(extra[:, :, E + 1], inv_g[:]))
                v.tensor_tensor(cnt[:], oh[:, :, 0, :], oh[:, :, 1, :], ALU.add).then_inc(s["top_ok"], 1)

            def carry_on(total, counts, n_e, ok_sem, n):
                own.link(v.tensor_reduce(out=csum[:, 0:n_e], in_=counts[:].bitcast(F32).rearrange("p g e -> p e g"), axis=AX.X, op=ALU.add))
                own.link(v.tensor_tensor(total[:, 0:n_e], total[:, 0:n_e].bitcast(F32), csum[:, 0:n_e], ALU.add))

            def one_pos(n, src, psem, rsem, dst):
                n.wait(s[psem], 1, 0)
                v.tensor_tensor(pm[:], oh[:], src.unsqueeze(2).to_broadcast([S, G, 2, E]), ALU.mult).then_inc(s[rsem], 1)
                n.wait(s[rsem], 1, 0)
                own.link(v.tensor_reduce(out=dst, in_=pm[:], axis=AX.X, op=ALU.add))

            def overflow(n):
                own.link(v.tensor_scalar(drop[:], pos[:], float(CAP), None, ALU.is_ge))
                own.link(v.tensor_reduce(out=ovf[:], in_=drop[:], axis=AX.X, op=ALU.max))
                own.link(v.tensor_scalar(keep[:], ovf[:], -1.0, 1.0, ALU.mult, ALU.add))
                own.put(v.tensor_copy(cnt2[:, :, E:E + 1], ovf[:].unsqueeze(2)))
                v.tensor_tensor(cnt2[:, :, 0:E], cnt[:].bitcast(F32), keep[:].unsqueeze(2).to_broadcast([S, G, E]),
                                ALU.mult).then_inc(s["cnt2_ok"], 1)
                own.wait()
                n.wait(s["cnt2_ok"], 1, 0)

            def slots(n):
                own.put(v.tensor_scalar(pen[:, :, 0:2], ovf[:].unsqueeze(2).to_broadcast([S, G, 2]), 16384.0, float(E * CAP), ALU.mult, ALU.add))
                own.put(v.tensor_scalar(pen[:, :, 2:3], keep[:].unsqueeze(2), 16384.0, float(E * CAP), ALU.mult, ALU.add))
                own.link(v.scalar_tensor_tensor(cpos[:], mi3[:], -float(CAP), cpos[:], ALU.mult, ALU.add))
                own.link(v.tensor_tensor(slot_i[:].rearrange("p (g c) -> p g c", c=3), cpos[:], pen[:], ALU.add))
                own.put(v.tensor_single_scalar(lc_i[:, 0, :], slot_i[:], 127, ALU.bitwise_and))
                own.link(v.tensor_single_scalar(lc_i[:, 1, :], slot_i[:], 7, ALU.logical_shift_right))
                own.link(v.tensor_copy(lc[:], lc_i[:]))
                n.wait(s["ex_ok"], 1, 0)
                exv = ex[:].rearrange("p (g e) -> p g e", e=E)
                own.put(v.tensor_tensor(wnum[:], exv, cnt2[:, :, 0:E].bitcast(F32), ALU.mult))
                own.link(v.tensor_reduce(out=den[:, 0, :], in_=exv, axis=AX.X, op=ALU.add))
                own.link(v.reciprocal(den[:, 1, :], den[:, 0, :]))
                own.link(v.tensor_scalar(den[:, 0, :], den[:, 1, :], tg[0:S, 1:2], None, ALU.mult))
                v.tensor_tensor(extra[:, :, 0:E], wnum[:], den[:, 0, :].unsqueeze(2).to_broadcast([S, G, E]),
                                ALU.mult).then_inc(s["wd_ok"], 1)

            def hots(n):
                for i in range(G * 3):
                    own.put(v.tensor_scalar(hot_lo[:, i, :], iota_f[0:S, :], lc[:, 0, i:i + 1], None, ALU.is_equal))
                    ins = v.tensor_scalar(hot_col[:, i, :], iota_f[0:S, 0:TABLE], lc[:, 1, i:i + 1], ids[:, i // 3:i // 3 + 1],
                                          ALU.is_equal, ALU.mult)
                    if i < G * 3 - 1:
                        own.put(ins)
                    else:
                        ins.then_inc(s["hot_ok"], 1)
                own.wait()
                n.wait(s["hot_ok"], 1, 0)

            def steps(j, only=range(4)):
                n = Counts(dve, j)
                for k in only:
                    if there(j, k, -1):
                        p, slot = (k - 1) % 2, (k - 1) % 4
                        n.wait(s["o_ps"], 4, k)
                        own.link(v.scalar_tensor_tensor(xb[:, p, :], bv_sb[:], ps_o[0:S, H:H + 1], x_sb[:, slot, :], ALU.mult, ALU.add))
                        n.wait(s["base_ok"], 4, k - 2)
                        v.tensor_tensor(x1[:, p, :], ps_o[0:S, 0:H], xb[:, p, :], ALU.add).then_inc(s["x1_ok"], 1)
                        n.wait(s["x1_ok"], 4, k)
                        own.link(v.bn_stats(stat2[:, p, :], x1[:, p, :]))
                        v.bn_aggr(mv2[:, p, :], stat2[:, p, :]).then_inc(s["st2"], 1)
                    if there(j, k, 1):
                        ctx_half(n, k, 1)
                    if there(j, k, 2):
                        stats1(n, k, 2)
                    if there(j, k, -1):
                        n.wait(s["rs3_ok"], 4, k)
                        n.wait(h_out[p], 32, 16 * ((k - 1) // 2))
                        v.tensor_scalar(h_sb[:, p, :], x1[:, p, :], mv2[:, p, 0:1], rs3[:, p, 0:1],
                                        ALU.subtract, ALU.mult).then_inc(s["h_ok"], 1)
                    if k == 0 and group_there(j, -2):
                        n.wait(s["tab_ps"], 1, -1)
                        v.tensor_tensor(table[:], table[:], r_tab, ALU.add).then_inc(s["tab_ok"], 1)
                    if k == 1 and group_there(j, -1):
                        one_pos(n, r_pos, "pos_ps", "pos_rd", pos[:])
                    if k == 2 and group_there(j, -1):
                        n.wait(s["pos2_ps"], 1, 0)
                        own.put(v.tensor_copy(cpos[:, :, 2:3], r_pos2[:, :, E:E + 1]))
                        one_pos(n, r_pos2[:, :, 0:E], "pos2_ps", "pos2_rd", cpos[:, :, 0:2])
                    if there(j, k, 2):
                        normal1(n, k, 2)
                    if k == 1 and group_there(j, -1):
                        overflow(n)
                        carry_on(carry, cnt, E, None, n)
                    if k == 2 and group_there(j, -1):
                        slots(n)
                        carry_on(carry2, cnt2, E2, None, n)
                    if k == 3 and group_there(j, -1):
                        hots(n)
                        own.link(v.tensor_scalar(ids[:], ids[:], float(G * S), None, ALU.add))
                    if there(j, k, -1):
                        n.wait(s["lg_ps"], 4, k)
                        v.tensor_copy(logit[:, (k - 1) % 4, :], r_logit).then_inc(s["lg_ok"], 1)
                    if k == 0 and group_there(j, -1):
                        n.wait(s["lg_ok"], 4, k)
                        n.wait(s["base_ok"], 4, k)
                        n.wait(s["ext_out"], 16, -16)
                        top2()
                own.restart()

            n = Counts(dve, 0)
            stats1(n, -2, 2)
            stats1(n, -1, 2)
            normal1(n, -2, 2)
            normal1(n, -1, 2)
            ctx_half(n, -1, 1)
            own.restart()
            groups(dve, steps)
            dve.wait_ge(s["tab_ps"], B // G)
            v.tensor_tensor(table[:], table[:], r_tab, ALU.add).then_inc(s["tab_ok"], 1)
            dve.wait_ge(s["tab_ok"], B // G)

            own.put(v.tensor_scalar(gidx[:], table[:], 1.0, -1.0, ALU.max, ALU.add))
            own.link(v.tensor_scalar(empty[:], table[:], 0.0, None, ALU.is_equal))
            own.link(v.tensor_tensor(empty[:].rearrange("p (u c) -> p u c", c=2), empty[:].rearrange("p (u c) -> p u c", c=2),
                                     dummy_f[:].unsqueeze(1).to_broadcast([128, TABLE // 2, 2]), ALU.mult))
            own.put(v.scalar_tensor_tensor(sidx[:], table[:], -1.0, empty[:], ALU.add, ALU.add))
            dve.wait_ge(s["tot_ps"], 1)
            own.link(v.tensor_scalar(tot_i[:], r_tot[0:1, 0:E + 1], float(UNIT - 1), None, ALU.add))
            own.link(v.tensor_single_scalar(tot_i[:], tot_i[:], 8, ALU.logical_shift_right))
            own.link(v.tensor_scalar(nun[:], tot_i[:], 1.0, None, ALU.max))
            own.put(v.memset(cum[:], 0.0))
            own.wait()
            for e in range(E + 1):
                own.link(v.tensor_tensor(cum[:, e + 1:e + 2], cum[:, e:e + 1], nun[:, e:e + 1], ALU.add))
            own.put(v.tensor_copy(cum_i[:], cum[:]))
            own.link(v.tensor_scalar(step8[:], nun[:, 0:E], -2.0, float(CAP // 128), ALU.mult, ALU.add))
            own.link(v.tensor_tensor(ucol3[:], iota_f[0:1, 0:UNITS].unsqueeze(2).to_broadcast([1, UNITS, E]),
                                     cum[:, 1:E + 1].unsqueeze(1).to_broadcast([1, UNITS, E]), ALU.is_ge))
            own.link(v.tensor_tensor(ucol3[:], ucol3[:], step8[:].unsqueeze(1).to_broadcast([1, UNITS, E]), ALU.mult))
            own.link(v.tensor_reduce(out=ucol_f[:], in_=ucol3[:], axis=AX.X, op=ALU.add))
            own.link(v.scalar_tensor_tensor(ucol[:], iota_f[0:1, 0:UNITS], 2.0, ucol_f[:], ALU.mult, ALU.add))
            own.restart()
            dve.sem_inc(s["plan_ok"], 1)

            def unit(g, e, ft):
                res = W_INV if ft > 1 else W_NONE
                g1 = dve.snap(g + 1)
                g16 = dve.snap(g * 16 + 16)
                for i in range(2):
                    dve.wait_ge(hg_in[i], g16)
                    own.put(v.tensor_copy(w_now[:, i:i + 1], hg[i][:, bass.ds(e + H, 1)]))
                own.wait()
                own.put(v.tensor_tensor(wi_now[:, 0:1], w_now[:, 0:1], hg[0][:, res:res + 1], ALU.mult))
                v.tensor_tensor(wi_now[:, 1:2], w_now[:, 1:2], hg[1][:, res:res + 1], ALU.mult).then_inc(s["wi_ok"], 1)
                dve.wait_ge(s["gT_ps"], g1)
                own.put(v.tensor_scalar(hgT[:, 0, :], bank[0][:, 0:UNIT], norm_now[:, 0:1], None, ALU.mult))
                own.wait()
                v.tensor_scalar(hgT[:, 1, :], bank[0][:, UNIT:2 * UNIT], norm_now[:, 1:2], None, ALU.mult).then_inc(s["gT_ok"], 1)
                for f in range(ft):
                    dve.wait_ge(gel_ok[f], g1)
                    dve.wait_ge(up_ps[f], g1)
                    v.tensor_tensor(act[:, f, :], gel[:, f % 2, :], bank[3 + f % 2][:, 0:UNIT], ALU.mult).then_inc(act_ok[f], 1)
                dve.wait_ge(s["yo_free"], g1)
                dve.wait_ge(s["hw_ok"], g1)
                dve.wait_ge(s["dn_ps"], g1)
                own.put(v.scalar_tensor_tensor(yo[:, 0, :], bank[5][:, 0:H], w_now[:, 0:1], hw[:, 0, :], ALU.mult, ALU.add))
                own.wait()
                v.scalar_tensor_tensor(yo[:, 1, :], bank[6][:, 0:H], w_now[:, 1:2], hw[:, 1, :], ALU.mult, ALU.add).then_inc(s["yo_ok"], 1)
                dve.wait_ge(s["yo_ok"], dve.snap(g + 2))
                settle(dve, s["settled"])
                own.restart()

            with dve.Fori(0, E) as e:
                own.link(v.tensor_copy(norm_now[:], norms_sb[:, bass.ds(e, 1), :].rearrange("p o k -> p (o k)")))
                own.restart()
                lo = dve.value_load(cum_i[0:1, bass.ds(e, 1)], min_val=0, max_val=UNITS - 2)
                hi = dve.value_load(cum_i[0:1, bass.ds(e + 1, 1)], min_val=1, max_val=UNITS - 2)
                with dve.Fori(lo, hi) as g:
                    unit(g, e, 4)
            own.link(v.tensor_copy(norm_now[:], norms_sb[:, E, :]))
            own.restart()
            lo = dve.value_load(cum_i[0:1, E:E + 1], min_val=E, max_val=UNITS - 2)
            hi = dve.value_load(cum_i[0:1, E + 1:E + 2], min_val=E + 1, max_val=UNITS - 1)
            with dve.Fori(lo, hi) as g:
                unit(g, E, 1)

        @block.tensor
        def _(pe):
            t = nc.tensor

            def mm(o, l, r, first, last):
                return t.matmul(o, l, r, start=first, stop=last)

            def transposes(n, k, off):
                slot, p, c = (k + off) % 4, (k + off) % 2, k + off + 1
                n.wait(s["y_ok"], 4, c)
                n.wait(s["qp_ok"], 4, c - 1)
                for h in range(2):
                    last = t.transpose(ps_q[:, h * S:(h + 1) * S], y_sb[:, p, h * 128:(h + 1) * 128], ident[0:S, 0:S])
                last.then_inc(s["yT_ps"], 1)
                n.wait(ctx_in[slot], 32, 32 * ((k + off) // 4 + 1))
                for h, bk_ in enumerate((ps_c0, ps_c1)):
                    n.wait(s[f"c{h}_ok"], 4, c - 1)
                    for i in range(3):
                        last = t.transpose(bk_[:, i * KC:(i + 1) * KC], ctx_sb[:, slot, i, h * 128:(h + 1) * 128], ident[0:KC, 0:KC])
                    last.then_inc(s[f"c{h}_ps"], 1)

            def projections(n, k, off):
                c = k + off + 1
                n.wait(s["c0_ok"], 4, c)
                n.wait(s["c1_ok"], 4, c)
                n.wait(s["kp_ok"], 4, c - 1)
                for h in range(2):
                    last = mm(ps_k[0:QK, 0:C], wk_sb[:, h, :], ctxT[:, h, :], h == 0, h == 1)
                last.then_inc(s["kp_ps"], 1)
                n.wait(s["yT_ok"], 4, c)
                for h in range(2):
                    last = mm(ps_q[0:QK, 2 * S:3 * S], wq_sb[:, h, :], yT[:, h, :], h == 0, h == 1)
                last.then_inc(s["qp_ps"], 1)

            def ranks(n, dst, counts, total, n_e, ok, ps):
                n.wait(s[ok], 1, 0)
                mm(dst, before_r[:], counts[:], True, False)
                for i in range(G - 1):
                    mm(dst[:, i + 1:G, :], ones_r[:, 0:S], counts[:, i, :].unsqueeze(1).to_broadcast([S, G - 1 - i, n_e]), False, False)
                mm(dst, ones_r[:, 0:S], total[:, 0:n_e].unsqueeze(1).to_broadcast([S, G, n_e]), False, True).then_inc(s[ps], 1)

            def steps(j, only=range(4)):
                n = Counts(pe, j)
                for k in only:
                    if there(j, k, 0):
                        n.wait(s["kp_ok"], 4, k + 1)
                        n.wait(s["qp_ok"], 4, k + 1)
                        n.wait(s["z_ok"], 4, k)
                        for i in range(3):
                            last = mm(ps_s[0:KC, i * S:(i + 1) * S], kpT[:, i * KC:(i + 1) * KC], qpT[:], True, True)
                        last.then_inc(s["s_ps"], 1)
                    if there(j, k, -1):
                        p = (k - 1) % 2
                        n.wait(s["av_ok"], 4, k)
                        n.wait(s["x1_ok"], 4, k - 1)
                        for h in range(2):
                            mm(ps_o[0:S, 0:H], avT[:, h, :], wv_sb[:, h, :], h == 0, h == 1)
                        for i in range(3):
                            last = mm(ps_o[0:S, H:H + 1], z_sb[:, p, i, :], ones[0:KC, 0:1], i == 0, i == 2)
                        last.then_inc(s["o_ps"], 1)
                    if there(j, k, 1):
                        transposes(n, k, 1)
                    if there(j, k, 0):
                        slot = k % 4
                        n.wait(s["z_ok"], 4, k + 1)
                        n.wait(s["hT_ok"], 4, k - 1)
                        for h in range(2):
                            for i in range(3):
                                last = mm(ps_v[:, h * S:(h + 1) * S], ctx_sb[:, slot, i, h * 128:(h + 1) * 128],
                                          z_sb[:, k % 2, i, :], i == 0, i == 2)
                        last.then_inc(s["av_ps"], 1)
                    if k < 3 and group_there(j, -2 if k == 0 else -1):
                        n.wait(s["lg_ok"], 4, min(k - 1, 0 if isinstance(j, int) and j > LAST else 9))
                    if k == 0 and group_there(j, -2):
                        n.wait(s["hot_ok"], 1, -1)
                        for i in range(3 * G):
                            last = mm(r_tab, hot_lo[:, i, :], hot_col[:, i, :], i == 0, i == 3 * G - 1)
                        last.then_inc(s["tab_ps"], 1)
                    if k == 1 and group_there(j, -1):
                        ranks(n, r_pos, cnt, carry, E, "top_ok", "pos_ps")
                    if k == 2 and group_there(j, -1):
                        ranks(n, r_pos2, cnt2, carry2, E2, "cnt2_ok", "pos2_ps")
                    if there(j, k, 1):
                        projections(n, k, 1)
                    if there(j, k, -1):
                        p = (k - 1) % 2
                        n.wait(s["h_ok"], 4, k)
                        if there(j, k, 0):
                            n.wait(s["av_ok"], 4, k + 1)
                        for h in range(2):
                            last = t.transpose(ps_v[:, (2 + h) * S:(3 + h) * S], h_sb[:, p, h * 128:(h + 1) * 128], ident[0:S, 0:S])
                        last.then_inc(s["hT_ps"], 1)
                        n.wait(s["hT_ok"], 4, k)
                        n.wait(s["lg_ok"], 4, k - 1)
                        if k == 0 and group_there(j, -2):
                            n.wait(s["tab_ok"], 1, -1)
                        if k == 1 and group_there(j, -1):
                            n.wait(s["pos_rd"], 1, 0)
                        if k == 2 and group_there(j, -1):
                            n.wait(s["pos2_rd"], 1, 0)
                        for h in range(2):
                            last = mm(r_logit, hT[:, h, :], wr_sb[:, h, :], h == 0, h == 1)
                        last.then_inc(s["lg_ps"], 1)

            pe.wait_ge(s["c_dve"], 1)
            pe.wait_ge(s["c_tanh"], 3)
            n = Counts(pe, 0)
            transposes(n, -1, 1)
            projections(n, -1, 1)
            groups(pe, steps)
            pe.wait_ge(s["hot_ok"], B // G)
            for i in range(3 * G):
                last = mm(r_tab, hot_lo[:, i, :], hot_col[:, i, :], i == 0, i == 3 * G - 1)
            last.then_inc(s["tab_ps"], 1)
            pe.wait_ge(s["tab_ok"], B // G)
            mm(r_tot[:, 0:E + 1], ones[0:S, :], carry2[:, 0:E + 1].bitcast(F32), True, True).then_inc(s["tot_ps"], 1)
            pe.wait_ge(s["plan_ok"], 1)

            def unit(g, ft, wgt):
                g1 = pe.snap(g + 1)
                g16 = pe.snap(g * 16 + 16)
                gw, uw, dw = wgt
                for i in range(2):
                    pe.wait_ge(hg_in[i], g16)
                    for h in range(2):
                        last = t.transpose(bank[0][:, h * UNIT + i * 128:h * UNIT + (i + 1) * 128],
                                           hg[i][:, h * 128:(h + 1) * 128], ident[:])
                last.then_inc(s["gT_ps"], 1)
                pe.wait_ge(s["gT_ok"], g1)
                for f in range(ft):
                    if f >= 2:
                        pe.wait_ge(act_ok[f - 2], g1)
                    for w, bk_, done in ((gw, bank[1 + f % 2], gate_ps[f]), (uw, bank[3 + f % 2], up_ps[f])):
                        for h in range(2):
                            last = mm(bk_[:, 0:UNIT], w[:, h, f * 128:(f + 1) * 128], hgT[:, h, :], h == 0, h == 1)
                        last.then_inc(done, 1)
                pe.wait_ge(s["yo_ok"], g1)
                order = [(f, i) for f in range(max(ft - 1, 0)) for i in range(2)] + [(ft - 1, i) for i in range(2)]
                for f, i in order:
                    pe.wait_ge(act_ok[f], g1)
                    last = mm(bank[5 + i][:, 0:H], act[:, f, i * 128:(i + 1) * 128], dw[:, f, :], f == 0, f == ft - 1)
                last.then_inc(s["dn_ps"], 1)

            with pe.Fori(0, E // 2) as i2:
                for q in range(2):
                    lo = pe.value_load(cum_i[0:1, bass.ds(i2 * 2 + q, 1)], min_val=0, max_val=UNITS - 2)
                    hi = pe.value_load(cum_i[0:1, bass.ds(i2 * 2 + (q + 1), 1)], min_val=1, max_val=UNITS - 2)
                    pe.wait_ge(s[f"w_in{q}"], pe.snap(i2 * 48 + 48))
                    settle(pe, s["settled"])
                    with pe.Fori(lo, hi) as g:
                        unit(g, 4, (wg_sb[q], wu_sb[q], wd_sb[q]))
                    pe.drain().then_inc(s["exp_done"], 1)
            pe.wait_ge(s["fw_in"], 48)
            lo = pe.value_load(cum_i[0:1, E:E + 1], min_val=E, max_val=UNITS - 2)
            hi = pe.value_load(cum_i[0:1, E + 1:E + 2], min_val=E + 1, max_val=UNITS - 1)
            with pe.Fori(lo, hi) as g:
                unit(g, 1, (fwg_sb, fwu_sb, fwd_sb))


def kernel(**inputs):
    import numpy as _np
    import concourse.bacc as _bacc
    from concourse.bass_utils import run_bass_kernel_spmd as _run

    a = {k: _np.asarray(v) for k, v in inputs.items()}
    norms = _np.concatenate([a["L0_ffn_norm_w"], a["L0_ffn_f_norm"][None]], 0)
    arrays = {
        "x": a["x"].reshape(N, H),
        "ctx_rows": a["ctx_1024"].reshape(B * C, H),
        "g2": _np.concatenate([a["g_xattn"], a["g_ffn"]]),
        "wqT": a["L0_xattn_Wq"].T, "bq": a["L0_xattn_bq"],
        "wkT": a["L0_xattn_Wk"].T, "bk": a["L0_xattn_bk"],
        "wvT": a["L0_xattn_Wv"].T, "bv": a["L0_xattn_bv"],
        "wr": a["L0_ffn_Wr"],
        "norms": norms.reshape(E + 1, 2, 128).transpose(2, 0, 1),
        "wg": a["L0_ffn_Wg"], "wu": a["L0_ffn_Wu"], "wd": a["L0_ffn_Wd"],
        "fwg": a["L0_ffn_fWg"], "fwu": a["L0_ffn_fWu"], "fwd": a["L0_ffn_fWd"],
    }
    arrays = {k: _np.ascontiguousarray(v) for k, v in arrays.items()}
    nc = _bacc.Bacc("TRN2", target_bir_lowering=False, num_devices=1)
    args = [nc.dram_tensor(k, v.shape, mybir.dt.from_np(v.dtype), kind="ExternalInput").ap() for k, v in arrays.items()]
    out = nc.dram_tensor("out", [N + DUMMY, H], F32, kind="ExternalOutput").ap()
    build(nc, *args, out)
    r = _run(nc, [arrays], core_ids=[0])
    return r.results[0]["out"][:N].reshape(B, S, H)
```

```python
import numpy as np
import concourse.bass as bass
from concourse import mybir
from contextlib import ExitStack

F32 = mybir.dt.float32
F32R = mybir.dt.float32r
I32 = mybir.dt.int32
U32 = mybir.dt.uint32
ALU = mybir.AluOpType
ACT = mybir.ActivationFunctionType
AX = mybir.AxisListType

B, S, H, C = 32, 112, 256, 375
KC = C // 3
QK = 64
E, F, FB = 8, 512, 128
E2 = E + 2
CAP = 1024
N = B * S
G = 4
UNIT = 256
COLS = E * CAP // 128
FCOLS = 32
TABLE = COLS + FCOLS
UNITS = 40
PAY = 272
W_FB, W_INV, W_NONE = H + E, H + E + 1, H + E + 2
DUMMY = UNIT
LN_EPS, RMS_EPS = 1e-5, 1e-6


class Chain:

    def __init__(self, engine, sem):
        self.engine, self.sem, self.n = engine, sem, 0

    def put(self, ins):
        ins.then_inc(self.sem, 1)
        self.n += 1

    def link(self, ins):
        self.put(ins)
        self.engine.wait_ge(self.sem, self.n)

    def wait(self):
        self.engine.wait_ge(self.sem, self.n)

    def restart(self):
        if self.n:
            self.engine.wait_ge(self.sem, self.n)
            self.engine.sem_clear(self.sem)
            self.n = 0


def settle(engine, sem):
    engine.sem_inc(sem, 1)


class Counts:

    def __init__(self, engine, j):
        self.engine, self.j, self.kept = engine, j, {}

    def __call__(self, a, c):
        if isinstance(self.j, int):
            return a * self.j + c
        if (a, c) not in self.kept:
            self.kept[a, c] = self.engine.snap(self.j * a + c)
        return self.kept[a, c]

    def wait(self, sem, a, c):
        v = self(a, c)
        if not isinstance(v, int) or v > 0:
            self.engine.wait_ge(sem, v)


def build(nc, x, ctx_rows, g2, wqT, bq, wkT, bk, wvT, bv, wr, norms, wg, wu, wd, fwg, fwu, fwd, out):
    stack = ExitStack()
    with stack:
        def sb(name, shape, dt=F32):
            return stack.enter_context(nc.sbuf_tensor(name, shape, dt))

        def sem(name):
            return stack.enter_context(nc.semaphore(name))

        payload = nc.dram_tensor("payload", [N, PAY], F32).ap()

        ident = sb("ident", [128, 128])
        before = sb("before", [S, S])
        ones = sb("ones", [128, 128])
        before_r = sb("before_r", [S, S], F32R)
        ones_r = sb("ones_r", [S, 128], F32R)
        iota_i = sb("iota_i", [128, 128], I32)
        iota_f = sb("iota_f", [128, 128])
        rev8 = sb("rev8", [S, E])
        ids = sb("ids", [S, G])
        ids_i = sb("ids_i", [S, G], I32)
        dummy_i = sb("dummy_i", [128, 2], I32)
        dummy_f = sb("dummy_f", [128, 2])
        zeros = sb("zeros", [128, 2 * H])
        exph = sb("exph", [S, 1])
        gate_copy = sb("gate_copy", [128, 2])
        gates = sb("gates", [128, 2])
        tg = sb("tg", [128, 2])
        wq_sb = sb("wq_sb", [128, 2, QK])
        wk_sb = sb("wk_sb", [128, 2, QK])
        wv_sb = sb("wv_sb", [128, 2, H])
        wr_sb = sb("wr_sb", [128, 2, E])
        bq_sb = sb("bq_sb", [QK, 1])
        bk_sb = sb("bk_sb", [QK, 1])
        bv_sb = sb("bv_sb", [KC, H])

        x_sb = sb("x_sb", [S, 4, H])
        ctx_sb = sb("ctx_sb", [KC, 4, 3, H])
        stat1 = sb("stat1", [S, 2, 6])
        mv1 = sb("mv1", [S, 2, 2])
        arg1 = sb("arg1", [S, 2, 1])
        rs1 = sb("rs1", [S, 2, 1])
        y_sb = sb("y_sb", [S, 2, H])
        yT = sb("yT", [128, 2, S])
        ctxT = sb("ctxT", [128, 2, C])
        kpT = sb("kpT", [QK, C])
        qpT = sb("qpT", [QK, S])
        z_sb = sb("z_sb", [KC, 2, 3, S])
        avT = sb("avT", [128, 2, S])
        x1 = sb("x1", [S, 2, H])
        stat2 = sb("stat2", [S, 2, 6])
        mv2 = sb("mv2", [S, 2, 2])
        arg3 = sb("arg3", [S, 2, 3])
        rs3 = sb("rs3", [S, 2, 3])
        ab = sb("ab", [S, 2, 3])
        h_sb = sb("h_sb", [S, 2, H])
        zs = sb("zs", [KC, S])
        inv_t = sb("inv_t", [S, 2, 1])
        base = sb("base", [S, 2, H])
        hT = sb("hT", [128, 2, S])
        logit = sb("logit", [S, G, E])
        inv_g = sb("inv_g", [S, G])
        m12 = sb("m12", [S, 2, G])
        eq = sb("eq", [S, G, E])
        rest = sb("rest", [S, G, E])
        mi3 = sb("mi3", [S, G, 3])
        oh = sb("oh", [S, G, 2, E])
        cnt = sb("cnt", [S, G, E], F32R)
        cnt2 = sb("cnt2", [S, G, E2], F32R)
        carry = sb("carry", [S, E2], F32R)
        carry2 = sb("carry2", [S, E2], F32R)
        csum = sb("csum", [S, E2])
        expo = sb("expo", [S, G * E])
        ex = sb("ex", [S, G * E])
        sg = sb("sg", [S, 2, G * E])
        den = sb("den", [S, 2, G])
        wnum = sb("wnum", [S, G, E])
        extra = sb("extra", [S, G, PAY - H])
        pm = sb("pm", [S, G, 2, E])
        pos = sb("pos", [S, G, 2])
        drop = sb("drop", [S, G, 2])
        ovf = sb("ovf", [S, G])
        keep = sb("keep", [S, G])
        cpos = sb("cpos", [S, G, 3])
        pen = sb("pen", [S, G, 3])
        slot_i = sb("slot_i", [S, G * 3], I32)
        lc_i = sb("lc_i", [S, 2, G * 3], I32)
        lc = sb("lc", [S, 2, G * 3])
        off = sb("off", [S, G * 3, 128])
        hot_lo = sb("hot_lo", [S, G * 3, 128], F32R)
        hot_col = sb("hot_col", [S, G * 3, TABLE], F32R)
        table = sb("table", [128, TABLE])
        gidx_f = sb("gidx_f", [128, TABLE])
        gidx = sb("gidx", [128, TABLE], I32)
        empty = sb("empty", [128, TABLE])
        sidx = sb("sidx", [128, TABLE], I32)
        tot_i = sb("tot_i", [128, E + 1], I32)
        nun = sb("nun", [128, E + 1])
        cum = sb("cum", [128, E + 2])
        cum_i = sb("cum_i", [128, E + 2], I32)
        step8 = sb("step8", [128, E])
        begun = sb("begun", [128, UNITS, E + 1])
        ucol3 = sb("ucol3", [128, UNITS, E])
        ucol_f = sb("ucol_f", [128, UNITS])
        ucol = sb("ucol", [128, UNITS], I32)
        uhot = sb("uhot", [128, UNITS, E + 1])
        raw_g = sb("raw_g", [128, 2, F])
        raw_u = sb("raw_u", [128, 2, F])
        raw_d = sb("raw_d", [128, 4, H])
        raw_n = sb("raw_n", [128, 2])
        wg_sb = [sb(f"wg_sb{q}", [128, 2, 2, F], F32R) for q in range(2)]
        wu_sb = [sb(f"wu_sb{q}", [128, 2, 2, F], F32R) for q in range(2)]
        wd_sb = [sb(f"wd_sb{q}", [128, 2, 4, H], F32R) for q in range(2)]
        gidx_now = sb("gidx_now", [128, 2], I32)
        sidx_now = sb("sidx_now", [128, 2], I32)
        sidx_u = sb("sidx_u", [128, UNITS, 2], I32)
        hg = sb("hg", [128, 2, PAY])
        w9 = sb("w9", [128, 2, E + 1])
        w_next = sb("w_next", [128, 2])
        w_now = sb("w_now", [128, 2])
        w_exp = sb("w_exp", [128, 2])
        wi_next = sb("wi_next", [128, 2])
        hw = sb("hw", [128, 4, H])
        hgT = sb("hgT", [128, 2, 2 * UNIT], F32R)
        gel = sb("gel", [128, 4, UNIT])
        prod = sb("prod", [128, 4, UNIT])
        act = sb("act", [128, 2, 4, UNIT], F32R)
        yo = sb("yo", [128, 2, H])

        bank = [stack.enter_context(nc.psum_tensor(f"bank{i}", [128, 512], F32)) for i in range(8)]
        ps_c0, ps_c1 = bank[0], bank[1]
        ps_q, ps_k, ps_s, ps_v, ps_o, ps_r = bank[2:8]
        r_logit = ps_r[0:S, 0:E]
        r_pos = ps_r[0:S, 32:32 + G * E].rearrange("p (g e) -> p g e", e=E)
        r_pos2 = ps_r[0:S, 64:64 + G * E2].rearrange("p (g e) -> p g e", e=E2)
        r_tab = ps_r[:, 128:128 + TABLE]
        r_tot = ps_s[:, 0:E + 2]

        names = ("const_in wts_in w_aff c_gp c_dve c_tanh dve_own act_own pool_own "
                 "st1 rs1_ok y_ok yT_ps c0_ps c1_ps yT_ok c0_ok c1_ok kp_ps qp_ps kp_ok qp_ok s_ps z_ok "
                 "av_ps av_ok o_ps x1_ok st2 rs3_ok h_ok base_ok zs_ok inv_ok inv_rd hT_ps hT_ok lg_ps lg_ok "
                 "top_ok ex_ok pos_ps pos_rd cnt2_ok pos2_ps pos2_rd wd_ok lc_ok hlo_ok hot_ok carried tab_ps tab_ok ext_out "
                 "tot_ps plan_ok rows_ok fill_out raw_gu raw_dn gu_hi gu_split wd_hi wd_split gT_ps gT_hi gT_ok wi_ok hw_ok yo_ok yo_free "
                 "dn_ps settled").split()
        s = {n: sem(n) for n in names}
        x_in = [sem(f"x_in{i}") for i in range(4)]
        ctx_in = [sem(f"ctx_in{i}") for i in range(4)]
        h_out = [sem(f"h_out{i}") for i in range(2)]
        base_out = [sem(f"base_out{i}") for i in range(2)]
        hg_in = [sem(f"hg_in{i}") for i in range(2)]
        added = [sem(f"added{i}") for i in range(2)]
        gu_ps = [sem(f"gu_ps{i}") for i in range(4)]
        gel_ok = [sem(f"gel_ok{i}") for i in range(4)]
        prod_ok = [sem(f"prod_ok{i}") for i in range(4)]
        hi_ok = [sem(f"hi_ok{i}") for i in range(4)]
        act_ok = [sem(f"act_ok{i}") for i in range(4)]

        LAST = B // G - 1
        N_CONST = 8

        def groups(engine, body, between=None, before_tail=None, first=0, loop=(2, 7), last=LAST + 3):
            for j in range(first, loop[0]):
                body(j)
            if between:
                between()
            with engine.Fori(loop[0], loop[1]) as j:
                body(j)
            if before_tail:
                before_tail()
            for j in range(loop[1], last):
                body(j)

        def there(j, k, off):
            return not isinstance(j, int) or 0 <= G * j + k + off < B

        def group_there(j, off):
            return not isinstance(j, int) or 0 <= j + off <= LAST

        block = stack.enter_context(nc.Block())

        @block.sync
        def _(sp):
            with nc.allow_non_contiguous_dma(reason="small constants"):
                sp.dma_start(gates[:], g2.rearrange("(o a) -> o a", o=1).to_broadcast([128, 2])).then_inc(s["const_in"], 16)
                sp.dma_start(bq_sb[:], bq.rearrange("(p o) -> p o", o=1)).then_inc(s["const_in"], 16)
                sp.dma_start(bk_sb[:], bk.rearrange("(p o) -> p o", o=1)).then_inc(s["const_in"], 16)
                sp.dma_start(bv_sb[:], bv.rearrange("(o a) -> o a", o=1).to_broadcast([KC, H])).then_inc(s["const_in"], 16)
            sp.dma_start(wv_sb[:], wvT.rearrange("(k p) d -> p k d", p=128)).then_inc(s["const_in"], 16)

            def load_x(row, slot):
                sp.dma_start(x_sb[:, slot, :], x[bass.ds(row, S), :]).then_inc(x_in[slot], 16)

            def load_ctx(ctx_row, slot):
                sp.dma_start(ctx_sb[0:S, slot],
                             ctx_rows[bass.ds(ctx_row, 3 * S), :].rearrange("(p c) d -> p c d", c=3)).then_inc(ctx_in[slot], 16)
                sp.dma_start(ctx_sb[S:KC, slot],
                             ctx_rows[bass.ds(ctx_row + 3 * S, C - 3 * S), :].rearrange("(p c) d -> p c d", c=3)).then_inc(ctx_in[slot], 16)

            load_x(0, 0)
            load_ctx(0, 0)
            sp.dma_start(wq_sb[:], wqT.rearrange("(k p) d -> p k d", p=128)).then_inc(s["const_in"], 16)
            sp.dma_start(wk_sb[:], wkT.rearrange("(k p) d -> p k d", p=128)).then_inc(s["const_in"], 16)
            sp.dma_start(wr_sb[:], wr.rearrange("(k p) d -> p k d", p=128)).then_inc(s["const_in"], 16)
            load_x(S, 1)
            load_ctx(C, 1)
            load_x(2 * S, 2)
            load_ctx(2 * C, 2)
            sp.wait_ge(s["c_gp"], 1)
            sp.dma_start(out[N:N + DUMMY, :].rearrange("(p c) d -> p (c d)", c=2), zeros[:]).then_inc(s["fill_out"], 16)

            def load_gate_up(src_g, src_u, src_n, width):
                sp.dma_start(raw_g[:, :, 0:width], src_g).then_inc(s["raw_gu"], 16)
                sp.dma_start(raw_u[:, :, 0:width], src_u).then_inc(s["raw_gu"], 16)
                with nc.allow_non_contiguous_dma(reason="8 B of a norm's weights per row"):
                    sp.dma_start(raw_n[:], src_n).then_inc(s["raw_gu"], 16)

            def expert_gate_up(e):
                load_gate_up(wg[bass.ds(e, 1)].rearrange("o (k p) f -> p (o k) f", p=128),
                             wu[bass.ds(e, 1)].rearrange("o (k p) f -> p (o k) f", p=128),
                             norms[:, bass.ds(e, 1), :].rearrange("p o k -> p (o k)"), F)

            def expert_down(e):
                sp.dma_start(raw_d[:], wd[bass.ds(e, 1)].rearrange("o (k p) d -> p (o k) d", p=128)).then_inc(s["raw_dn"], 16)

            def steps(j):
                n = Counts(sp, j)
                for k in range(4):
                    if there(j, k, 3):
                        n.wait(s["av_ps"], 4, k)
                        load_ctx(G * C * j + (k + 3) * C, (k + 3) % 4)
                        n.wait(s["x1_ok"], 4, k)
                        load_x(G * S * j + (k + 3) * S, (k + 3) % 4)
                    if there(j, k, -1):
                        row = G * S * j + (k - 1) * S
                        p = (k - 1) % 2
                        n.wait(s["h_ok"], 4, k)
                        sp.dma_start(payload[bass.ds(row, S), 0:H], h_sb[:, p, :]).then_inc(h_out[p], 16)
                        n.wait(s["base_ok"], 4, k)
                        sp.dma_start(out[bass.ds(row, S), :], base[:, p, :]).then_inc(base_out[p], 16)
                    if k == 0 and group_there(j, -2):
                        n.wait(s["wd_ok"], 1, -1)
                        with nc.allow_non_contiguous_dma(reason="64 B of weights per token"):
                            sp.dma_start(payload[bass.ds(G * S * (j - 2), G * S), H:PAY].rearrange("(g p) c -> p g c", g=G),
                                         extra[:]).then_inc(s["ext_out"], 16)

            def weights(e):
                if not isinstance(e, int) or e > 0:
                    sp.wait_ge(s["gu_split"], e)
                expert_gate_up(e)
                if not isinstance(e, int) or e > 0:
                    sp.wait_ge(s["wd_split"], e)
                expert_down(e)

            steps(0)
            weights(0)
            groups(sp, steps, before_tail=lambda: weights(1), first=1)
            with sp.Fori(2, E) as e:
                weights(e)
            sp.wait_ge(s["gu_split"], E)
            load_gate_up(fwg.rearrange("(k p) f -> p k f", p=128), fwu.rearrange("(k p) f -> p k f", p=128), norms[:, E, :], FB)
            sp.wait_ge(s["wd_split"], E)
            sp.dma_start(raw_d[:, 0, :], fwd).then_inc(s["raw_dn"], 16)
            for p in range(2):
                sp.wait_ge(base_out[p], 16 * B // 2)

        @block.gpsimd
        def _(pool):
            own = Chain(pool, s["pool_own"])
            gp = nc.gpsimd
            own.put(gp.memset(ones[:], 1.0))
            own.put(gp.iota(iota_i[:], [[1, 128]], 0, 0))
            own.put(gp.iota(ids_i[:], [[S, G]], 1 - G * S, 1))
            own.put(gp.iota(dummy_i[:], [[128, 2]], N + 1, 1))
            own.put(gp.memset(exph[:], -0.5))
            own.put(gp.memset(mi3[:], 0.0))
            own.put(gp.memset(extra[:], 0.0))
            own.put(gp.memset(table[:], 0.0))
            own.put(gp.memset(cnt2[:].bitcast(F32), 0.0))
            own.put(gp.memset(carry[:].bitcast(F32), 0.0))
            own.put(gp.memset(carry2[:].bitcast(F32), 0.0))
            own.link(gp.memset(zeros[:], 0.0))
            own.put(gp.affine_select(out=ident[:], in_=ones[:], compare_op=ALU.is_equal, fill=0.0, base=0,
                                     pattern=[[-1, 128]], channel_multiplier=1))
            own.link(gp.affine_select(out=before[:], in_=ones[0:S, 0:S], compare_op=ALU.is_gt, fill=0.0, base=0,
                                      pattern=[[1, S]], channel_multiplier=-1))
            pool.sem_inc(s["c_gp"], 1)
            pool.sem_inc(s["yo_free"], 1)
            pool.sem_inc(s["dn_ps"], 1)
            pool.wait_ge(s["c_tanh"], 3)

            def steps(j):
                n = Counts(pool, j)
                for k in range(4):
                    if there(j, k, 2):
                        p = k % 2
                        n.wait(s["st1"], 4, k + 3)
                        settle(pool, s["settled"])
                        own.link(gp.tensor_scalar(arg1[:, p, :], mv1[:, p, 1:2], 1.0, LN_EPS, ALU.mult, ALU.add))
                        gp.tensor_tensor(rs1[:, p, :], arg1[:, p, :], exph[:], ALU.pow).then_inc(s["rs1_ok"], 1)
                    if there(j, k, 0):
                        n.wait(s["z_ok"], 4, k + 1)
                        n.wait(s["o_ps"], 4, k)
                        own.link(gp.tensor_tensor(zs[:], z_sb[:, k % 2, 0, :], z_sb[:, k % 2, 1, :], ALU.add))
                        gp.tensor_tensor(zs[:], zs[:], z_sb[:, k % 2, 2, :], ALU.add).then_inc(s["zs_ok"], 1)
                    if there(j, k, -1):
                        p = (k - 1) % 2
                        n.wait(s["st2"], 4, k)
                        settle(pool, s["settled"])
                        own.link(gp.tensor_scalar(arg3[:, p, 0:1], mv2[:, p, 1:2], 1.0 + RMS_EPS, RMS_EPS * LN_EPS, ALU.mult, ALU.add))
                        gp.tensor_tensor(rs3[:, p, 0:1], arg3[:, p, 0:1], exph[:], ALU.pow).then_inc(s["rs3_ok"], 1)
                        own.link(gp.tensor_scalar(arg3[:, p, 1:2], mv2[:, p, 1:2], 1.0, LN_EPS, ALU.mult, ALU.add))
                        own.link(gp.tensor_tensor(rs3[:, p, 1:2], arg3[:, p, 1:2], exph[:], ALU.pow))
                        n.wait(s["rs3_ok"], 4, k)
                        own.put(gp.tensor_tensor(rs3[:, p, 2:3], arg3[:, p, 0:1], rs3[:, p, 0:1], ALU.mult))
                        own.put(gp.tensor_tensor(ab[:, p, 2:3], mv2[:, p, 0:1], rs3[:, p, 1:2], ALU.mult))
                        own.link(gp.tensor_scalar(ab[:, p, 0:1], rs3[:, p, 1:2], tg[0:S, 1:2], 1.0, ALU.mult, ALU.add))
                        own.link(gp.tensor_scalar(ab[:, p, 1:2], ab[:, p, 2:3], tg[0:S, 1:2], -1.0, ALU.mult, ALU.mult))
                        n.wait(s["inv_rd"], 4, k - 2)
                        gp.tensor_tensor(inv_t[:, p, :], rs3[:, p, 1:2], rs3[:, p, 2:3], ALU.mult).then_inc(s["inv_ok"], 1)
                        n.wait(base_out[p], 32, 16 * ((k - 1) // 2))
                        settle(pool, s["settled"])
                        gp.tensor_scalar(base[:, p, :], x1[:, p, :], ab[:, p, 0:1], ab[:, p, 1:2], ALU.mult, ALU.add).then_inc(s["base_ok"], 1)
                own.restart()

            for t in range(2):
                pool.wait_ge(s["st1"], t + 1)
                own.link(gp.tensor_scalar(arg1[:, t, :], mv1[:, t, 1:2], 1.0, LN_EPS, ALU.mult, ALU.add))
                gp.tensor_tensor(rs1[:, t, :], arg1[:, t, :], exph[:], ALU.pow).then_inc(s["rs1_ok"], 1)
            own.restart()
            groups(pool, steps)

            pool.wait_ge(s["plan_ok"], 1)
            pool.wait_ge(s["ext_out"], 16 * (B // G))
            pool.wait_ge(s["fill_out"], 16)
            for p in range(2):
                pool.wait_ge(h_out[p], 16 * B // 2)
                pool.wait_ge(base_out[p], 16 * B // 2)

            pool.wait_ge(s["rows_ok"], 1)

            def gather(u, col):
                own.link(gp.tensor_copy(gidx_now[:], gidx[:, bass.ds(col, 2)]))
                for i in range(2):
                    gp.indirect_dma_start(out=hg[:, i, :], out_offset=None, in_=payload,
                                          in_offset=bass.IndirectOffsetOnAxis(ap=gidx_now[:, i:i + 1], axis=0)).then_inc(hg_in[i], 16)
                own.put(gp.tensor_copy(sidx_u[:, bass.ds(u, 1), :].rearrange("p o c -> p (o c)"), sidx[:, bass.ds(col, 2)]))

            def ahead(u, parity):
                col = pool.value_load(ucol[0:1, bass.ds(u + 1, 1)], min_val=0, max_val=TABLE - 2)
                pool.wait_ge(s["wi_ok"], pool.snap(u + 1))
                settle(pool, s["settled"])
                gp.tensor_tensor(hw[:, bass.ds(parity * 2, 2), :], hg[:, :, 0:H], wi_next[:].unsqueeze(2).to_broadcast([128, 2, H]),
                                 ALU.mult).then_inc(s["hw_ok"], 1)
                pool.wait_ge(s["hw_ok"], pool.snap(u + 1))
                pool.wait_ge(s["gT_ps"], pool.snap(u + 1))
                gather(u + 1, col)

            def scatter(u):
                pool.wait_ge(s["yo_ok"], pool.snap(u + 2))
                own.link(gp.tensor_copy(sidx_now[:], sidx_u[:, bass.ds(u, 1), :].rearrange("p o c -> p (o c)")))
                for i in range(2):
                    gp.indirect_dma_start(out=out, out_offset=bass.IndirectOffsetOnAxis(ap=sidx_now[:, i:i + 1], axis=0),
                                          in_=yo[:, i, :], in_offset=None, compute_op=ALU.add).then_inc(added[i], 16)

            n_units = pool.value_load(cum_i[0:1, E + 1:E + 2], min_val=E + 1, max_val=UNITS - 3)
            col0 = pool.value_load(ucol[0:1, 0:1], min_val=0, max_val=TABLE - 2)
            gather(0, col0)
            own.restart()
            ahead(0, 0)
            ahead(1, 1)
            own.restart()
            with pool.Fori(1, n_units) as g:
                scatter(g - 1)
                ahead(g + 1, pool.snap((g + 1) & 1))
                g16 = pool.snap(g * 16)
                for i in range(2):
                    pool.wait_ge(added[i], g16)
                pool.sem_inc(s["yo_free"], 1)
                own.restart()
            scatter(n_units - 1)
            for i in range(2):
                pool.wait_ge(added[i], pool.snap(n_units * 16))
                pool.wait_ge(hg_in[i], pool.snap(n_units * 16 + 32))

        @block.scalar
        def _(act_e):
            sc = nc.scalar
            act_e.wait_ge(s["const_in"], 16 * N_CONST)
            sc.activation(tg[:], gates[:], ACT.Tanh).then_inc(s["c_tanh"], 1)
            act_e.wait_ge(s["c_tanh"], 1)
            sc.activation(wv_sb[:], wv_sb[:], ACT.Copy, scale=tg[:, 0:1]).then_inc(s["c_tanh"], 1)
            sc.activation(bv_sb[:], bv_sb[:], ACT.Copy, scale=tg[0:KC, 0:1]).then_inc(s["c_tanh"], 1)

            def head(n, k, off):
                c = k + off + 1
                n.wait(s["c0_ps"], 4, c)
                sc.activation(ctxT[:, 0, :], ps_c0[:, 0:C], ACT.Copy).then_inc(s["c0_ok"], 1)
                n.wait(s["c1_ps"], 4, c)
                sc.activation(ctxT[:, 1, :], ps_c1[:, 0:C], ACT.Copy).then_inc(s["c1_ok"], 1)
                n.wait(s["yT_ps"], 4, c)
                sc.activation(yT[:], ps_q[:, 0:2 * S].rearrange("p (k q) -> p k q", k=2), ACT.Copy).then_inc(s["yT_ok"], 1)

            def proj(n, k, off):
                c = k + off + 1
                n.wait(s["kp_ps"], 4, c)
                sc.activation(kpT[:], ps_k[0:QK, 0:C], ACT.Identity, bias=bk_sb[:]).then_inc(s["kp_ok"], 1)
                n.wait(s["qp_ps"], 4, c)
                sc.activation(qpT[:], ps_q[0:QK, 2 * S:3 * S], ACT.Identity, bias=bq_sb[:]).then_inc(s["qp_ok"], 1)

            def hot_rows(n, part):
                size = 3
                n.wait(s["lc_ok"], 1, -1)
                n.wait(s["tab_ps"], 1, -2)
                for i in range(part * size, (part + 1) * size):
                    last = sc.activation(off[:, i, :], iota_f[0:S, :], ACT.Abs, scale=-1.0, bias=lc[:, 0, i:i + 1])
                last.then_inc(s["act_own"], 1)
                n.wait(s["act_own"], 4, part - 7)
                sc.activation(hot_lo[:, part * size:(part + 1) * size, :], off[:, part * size:(part + 1) * size, :],
                              ACT.Relu, scale=-1.0, bias=ones[0:S, 0:1]).then_inc(s["hlo_ok"], 1)

            def steps(j):
                n = Counts(act_e, j)
                for k in range(4):
                    if there(j, k, 0):
                        n.wait(s["s_ps"], 4, k + 1)
                        n.wait(s["zs_ok"], 4, k - 1)
                        sc.activation(z_sb[:, k % 2], ps_s[0:KC, 0:3 * S].rearrange("p (c q) -> p c q", c=3),
                                      ACT.Sigmoid, scale=1.0 / float(np.sqrt(QK))).then_inc(s["z_ok"], 1)
                    if there(j, k, -2):
                        n.wait(s["hT_ps"], 4, k - 1)
                        sc.activation(hT[:], ps_v[:, 2 * S:4 * S].rearrange("p (k q) -> p k q", k=2), ACT.Copy).then_inc(s["hT_ok"], 1)
                    if k == 2 and group_there(j, -1):
                        n.wait(s["top_ok"], 1, 0)
                        sc.activation(sg[:, 0, :], expo[:], ACT.Sigmoid)
                        sc.activation(sg[:, 1, :], expo[:], ACT.Sigmoid, scale=-1.0).then_inc(s["ex_ok"], 1)
                    if k < 2 and group_there(j, -2):
                        hot_rows(n, 3 * k)
                    if there(j, k, 0):
                        n.wait(s["av_ps"], 4, k + 1)
                        sc.activation(avT[:], ps_v[:, 0:2 * S].rearrange("p (k q) -> p k q", k=2), ACT.Copy).then_inc(s["av_ok"], 1)
                    if k == 0 and group_there(j, -2):
                        hot_rows(n, 1)
                    if there(j, k, 1):
                        proj(n, k, 1)
                    if k == 0 and group_there(j, -2):
                        hot_rows(n, 2)
                    if there(j, k, 2):
                        head(n, k, 2)

            n = Counts(act_e, 0)
            head(n, -2, 2)
            proj(n, -1, 1)
            head(n, -1, 2)
            def split_gate_up(q, count):
                act_e.wait_ge(s["raw_gu"], count(48))
                for k in range(2):
                    for w, raw in ((wg_sb[q], raw_g), (wu_sb[q], raw_u)):
                        sc.activation(w[:, 0, k, :], raw[:, k, :], ACT.Copy, scale=raw_n[:, k:k + 1]).then_inc(s["gu_hi"], 1)

            def split_down(q, count):
                act_e.wait_ge(s["raw_dn"], count(16))
                sc.activation(wd_sb[q][:, 0], raw_d[:], ACT.Copy).then_inc(s["wd_hi"], 1)

            def split_first():
                split_gate_up(0, lambda m: m)
                split_down(0, lambda m: m)

            groups(act_e, steps, between=split_first)

            act_e.wait_ge(s["plan_ok"], 1)

            def next_hT(u1):
                act_e.wait_ge(s["gT_ps"], u1)
                sc.activation(hgT[:, 0, :], bank[0][:], ACT.Copy).then_inc(s["gT_hi"], 1)

            def unit(g, ft):
                g1 = act_e.snap(g + 1)

                def upper(f):
                    act_e.wait_ge(prod_ok[f], g1)
                    sc.activation(act[:, 0, f, :], prod[:, f, :], ACT.Copy).then_inc(hi_ok[f], 1)

                for f in range(ft):
                    act_e.wait_ge(gu_ps[f], g1)
                    sc.activation(gel[:, f, :], bank[1 + f][:, 0:UNIT], ACT.Gelu).then_inc(gel_ok[f], 1)
                    if f > 0:
                        upper(f - 1)
                upper(ft - 1)
                next_hT(act_e.snap(g + 2))

            next_hT(1)
            with act_e.Fori(0, E // 2) as i2:
                for q in range(2):
                    if q == 0:
                        lo = act_e.value_load(cum_i[0:1, bass.ds(i2 * 2, 1)], min_val=0, max_val=UNITS - 3)
                    hi = act_e.value_load(cum_i[0:1, bass.ds(i2 * 2 + (q + 1), 1)], min_val=1, max_val=UNITS - 3)
                    count = lambda m: act_e.snap(i2 * (2 * m) + (q + 2) * m)
                    if q == 0:
                        sc.activation(gate_copy[:], gates[:], ACT.Gelu)
                    act_e.wait_ge(s["dn_ps"], act_e.snap(lo + 1))
                    split_gate_up(1 - q, count)
                    with act_e.Fori(lo, hi) as g:
                        unit(g, 4)
                    split_down(1 - q, count)
                    lo = hi
            lo = act_e.value_load(cum_i[0:1, E:E + 1], min_val=E, max_val=UNITS - 3)
            hi = act_e.value_load(cum_i[0:1, E + 1:E + 2], min_val=E + 1, max_val=UNITS - 3)
            with act_e.Fori(lo, hi) as g:
                unit(g, 1)

        @block.vector
        def _(dve):
            own = Chain(dve, s["dve_own"])
            v = nc.vector
            dve.sem_inc(s["yo_ok"], 1)
            dve.wait_ge(s["c_gp"], 1)
            own.put(v.tensor_copy(before_r[:], before[:]))
            own.put(v.tensor_copy(ones_r[:], ones[0:S, :]))
            own.put(v.tensor_copy(ids[:], ids_i[:]))
            own.put(v.tensor_copy(dummy_f[:], dummy_i[:]))
            own.link(v.tensor_copy(iota_f[:], iota_i[:]))
            own.put(v.tensor_scalar(rev8[:], iota_f[0:S, 0:E], -1.0, float(E), ALU.mult, ALU.add))
            dve.wait_ge(s["c_tanh"], 3)
            own.put(v.tensor_copy(extra[:, :, E:E + 1], tg[0:S, 1:2].unsqueeze(1).to_broadcast([S, G, 1])))
            own.wait()
            dve.sem_inc(s["c_dve"], 1)

            def stats1(n, k, off):
                slot, p = (k + off) % 4, (k + off) % 2
                n.wait(x_in[slot], 16, 16 * ((k + off) // 4 + 1))
                own.link(v.bn_stats(stat1[:, p, :], x_sb[:, slot, :]))
                v.bn_aggr(mv1[:, p, :], stat1[:, p, :]).then_inc(s["st1"], 1)

            def normal1(n, k, off):
                slot, p = (k + off) % 4, (k + off) % 2
                n.wait(s["rs1_ok"], 4, k + off + 1)
                n.wait(s["yT_ps"], 4, k + off - 1)
                v.tensor_scalar(y_sb[:, p, :], x_sb[:, slot, :], mv1[:, p, 0:1], rs1[:, p, :],
                                ALU.subtract, ALU.mult).then_inc(s["y_ok"], 1)

            def top2():
                rev = rev8[:].unsqueeze(1).to_broadcast([S, G, E])
                own.link(v.tensor_reduce(out=m12[:, 0, :], in_=logit[:], axis=AX.X, op=ALU.max))
                src = logit
                for i in range(2):
                    mx = m12[:, i, :].unsqueeze(2).to_broadcast([S, G, E])
                    own.link(v.tensor_tensor(eq[:], src[:], mx, ALU.is_equal))
                    own.link(v.tensor_tensor(eq[:], eq[:], rev, ALU.mult))
                    own.link(v.tensor_reduce(out=mi3[:, :, i], in_=eq[:], axis=AX.X, op=ALU.max))
                    own.link(v.tensor_tensor(oh[:, :, i, :], rev, mi3[:, :, i:i + 1].to_broadcast([S, G, E]), ALU.is_equal))
                    if i == 0:
                        own.link(v.scalar_tensor_tensor(rest[:], oh[:, :, 0, :], -1e30, logit[:], ALU.mult, ALU.add))
                        own.link(v.tensor_reduce(out=m12[:, 1, :], in_=rest[:], axis=AX.X, op=ALU.max))
                        src = rest
                own.link(v.tensor_tensor(rest[:], logit[:], m12[:, 0, :].unsqueeze(2).to_broadcast([S, G, E]), ALU.subtract))
                own.put(v.tensor_tensor(expo[:].rearrange("p (g e) -> p g e", e=E), rest[:],
                                        inv_g[:].unsqueeze(2).to_broadcast([S, G, E]), ALU.mult))
                own.link(v.tensor_copy(extra[:, :, E + 1], inv_g[:]))
                v.tensor_tensor(cnt[:], oh[:, :, 0, :], oh[:, :, 1, :], ALU.add).then_inc(s["top_ok"], 1)

            def carry_on(total, counts, n_e, ok_sem, n):
                own.link(v.tensor_reduce(out=csum[:, 0:n_e], in_=counts[:].bitcast(F32).rearrange("p g e -> p e g"), axis=AX.X, op=ALU.add))
                own.link(v.tensor_tensor(total[:, 0:n_e], total[:, 0:n_e].bitcast(F32), csum[:, 0:n_e], ALU.add))

            def one_pos(n, src, psem, rsem, dst):
                n.wait(s[psem], 1, 0)
                v.tensor_tensor(pm[:], oh[:], src.unsqueeze(2).to_broadcast([S, G, 2, E]), ALU.mult).then_inc(s[rsem], 1)
                n.wait(s[rsem], 1, 0)
                own.link(v.tensor_reduce(out=dst, in_=pm[:], axis=AX.X, op=ALU.add))

            def overflow(n):
                own.link(v.tensor_scalar(drop[:], pos[:], float(CAP), None, ALU.is_ge))
                own.link(v.tensor_reduce(out=ovf[:], in_=drop[:], axis=AX.X, op=ALU.max))
                own.link(v.tensor_scalar(keep[:], ovf[:], -1.0, 1.0, ALU.mult, ALU.add))
                own.put(v.tensor_copy(cnt2[:, :, E:E + 1], ovf[:].unsqueeze(2)))
                v.tensor_tensor(cnt2[:, :, 0:E], cnt[:].bitcast(F32), keep[:].unsqueeze(2).to_broadcast([S, G, E]),
                                ALU.mult).then_inc(s["cnt2_ok"], 1)
                own.wait()
                n.wait(s["cnt2_ok"], 1, 0)

            def slots(n):
                own.put(v.tensor_scalar(pen[:, :, 0:2], ovf[:].unsqueeze(2).to_broadcast([S, G, 2]), 16384.0, float(E * CAP), ALU.mult, ALU.add))
                own.put(v.tensor_scalar(pen[:, :, 2:3], keep[:].unsqueeze(2), 16384.0, float(E * CAP), ALU.mult, ALU.add))
                own.link(v.scalar_tensor_tensor(cpos[:], mi3[:], -float(CAP), cpos[:], ALU.mult, ALU.add))
                own.link(v.tensor_tensor(slot_i[:].rearrange("p (g c) -> p g c", c=3), cpos[:], pen[:], ALU.add))
                own.put(v.tensor_single_scalar(lc_i[:, 0, :], slot_i[:], 127, ALU.bitwise_and))
                own.link(v.tensor_single_scalar(lc_i[:, 1, :], slot_i[:], 7, ALU.logical_shift_right))
                v.tensor_copy(lc[:], lc_i[:]).then_inc(s["lc_ok"], 1)

            def weights(n):
                n.wait(s["ex_ok"], 1, 0)
                own.link(v.reciprocal(ex[:], sg[:, 1, :]))
                own.link(v.tensor_tensor(ex[:], ex[:], sg[:, 0, :], ALU.mult))
                exv = ex[:].rearrange("p (g e) -> p g e", e=E)
                own.put(v.tensor_tensor(wnum[:], exv, cnt2[:, :, 0:E].bitcast(F32), ALU.mult))
                own.link(v.tensor_reduce(out=den[:, 0, :], in_=exv, axis=AX.X, op=ALU.add))
                own.link(v.reciprocal(den[:, 1, :], den[:, 0, :]))
                own.link(v.tensor_scalar(den[:, 0, :], den[:, 1, :], tg[0:S, 1:2], None, ALU.mult))
                v.tensor_tensor(extra[:, :, 0:E], wnum[:], den[:, 0, :].unsqueeze(2).to_broadcast([S, G, E]),
                                ALU.mult).then_inc(s["wd_ok"], 1)

            def hots(n, part):
                for i in part:
                    ins = v.tensor_scalar(hot_col[:, i, :], iota_f[0:S, 0:TABLE], lc[:, 1, i:i + 1], ids[:, i // 3:i // 3 + 1],
                                          ALU.is_equal, ALU.mult)
                    if i < G * 3 - 1:
                        own.put(ins)
                    else:
                        ins.then_inc(s["hot_ok"], 1)

            def add_table(n):
                n.wait(s["tab_ps"], 1, -1)
                v.tensor_tensor(table[:], table[:], r_tab, ALU.add).then_inc(s["tab_ok"], 1)

            def next_ids(n):
                own.link(v.tensor_scalar(ids[:], ids[:], float(G * S), None, ALU.add))

            def steps(j):
                n = Counts(dve, j)
                tail = isinstance(j, int) and j > LAST
                for k in range(4):
                    if there(j, k, 2):
                        stats1(n, k, 2)
                    if there(j, k, -1):
                        p, slot = (k - 1) % 2, (k - 1) % 4
                        n.wait(s["o_ps"], 4, k)
                        n.wait(s["base_ok"], 4, k - 2)
                        v.tensor_tensor(x1[:, p, :], ps_o[0:S, 0:H], x_sb[:, slot, :], ALU.add).then_inc(s["x1_ok"], 1)
                        n.wait(s["x1_ok"], 4, k)
                        own.link(v.bn_stats(stat2[:, p, :], x1[:, p, :]))
                        v.bn_aggr(mv2[:, p, :], stat2[:, p, :]).then_inc(s["st2"], 1)
                        if k == 0 and tail:
                            n.wait(s["lc_ok"], 1, -1)
                            next_ids(n)
                            hots(n, range(0, 4))
                    if k == 1 and group_there(j, -2) and not tail:
                        add_table(n)
                    if k == 2 and group_there(j, -1):
                        one_pos(n, r_pos, "pos_ps", "pos_rd", pos[:])
                        overflow(n)
                    if k == 3 and group_there(j, -1):
                        n.wait(s["pos2_ps"], 1, 0)
                        own.put(v.tensor_copy(cpos[:, :, 2:3], r_pos2[:, :, E:E + 1]))
                        one_pos(n, r_pos2[:, :, 0:E], "pos2_ps", "pos2_rd", cpos[:, :, 0:2])
                    if there(j, k, 2):
                        normal1(n, k, 2)
                    if there(j, k, -1):
                        n.wait(s["rs3_ok"], 4, k)
                        n.wait(h_out[p], 32, 16 * ((k - 1) // 2))
                        v.tensor_scalar(h_sb[:, p, :], x1[:, p, :], mv2[:, p, 0:1], rs3[:, p, 0:1],
                                        ALU.subtract, ALU.mult).then_inc(s["h_ok"], 1)
                    if k == 2 and group_there(j, -1):
                        carry_on(carry, cnt, E, None, n)
                    if k == 3 and group_there(j, -1):
                        slots(n)
                        carry_on(carry2, cnt2, E2, None, n)
                        if tail:
                            dve.sem_inc(s["carried"], 1)
                            dve.wait_ge(s["lc_ok"], B // G)
                            next_ids(n)
                            hots(n, range(3 * G))
                        weights(n)
                    if k == 0 and group_there(j, -2) and not tail:
                        n.wait(s["lc_ok"], 1, -1)
                        next_ids(n)
                        hots(n, range(3 * G))
                    if there(j, k, -2):
                        p = k % 2
                        n.wait(s["inv_ok"], 4, k - 1)
                        v.tensor_copy(inv_g[:, (k - 2) % 4:(k - 2) % 4 + 1], inv_t[:, p, :]).then_inc(s["inv_rd"], 1)
                        n.wait(s["lg_ps"], 4, k - 1)
                        v.tensor_copy(logit[:, (k - 2) % 4, :], r_logit).then_inc(s["lg_ok"], 1)
                        if k == 0 and tail:
                            hots(n, range(4, 3 * G))
                    if k == 1 and group_there(j, -1):
                        n.wait(s["lg_ok"], 4, k - 1)
                        n.wait(s["inv_rd"], 4, k - 1)
                        n.wait(s["ext_out"], 16, -16)
                        top2()
                        if tail:
                            add_table(n)
                own.restart()

            n = Counts(dve, 0)
            stats1(n, -2, 2)
            stats1(n, -1, 2)
            normal1(n, -2, 2)
            normal1(n, -1, 2)
            own.restart()
            def split_gate_up(q, count):
                for k in range(2):
                    for i, (w, raw) in enumerate(((wg_sb[q], raw_g), (wu_sb[q], raw_u))):
                        dve.wait_ge(s["gu_hi"], count(4, 2 * k + i - 3))
                        last = v.scalar_tensor_tensor(w[:, 1, k, :], raw[:, k, :], raw_n[:, k:k + 1],
                                                      w[:, 0, k, :].bitcast(F32), ALU.mult, ALU.subtract)
                        if (k, i) != (1, 1):
                            own.put(last)
                own.wait()
                last.then_inc(s["gu_split"], 1)

            def split_down(q, count):
                dve.wait_ge(s["wd_hi"], count(1, 0))
                v.tensor_tensor(wd_sb[q][:, 1], raw_d[:], wd_sb[q][:, 0].bitcast(F32), ALU.subtract).then_inc(s["wd_split"], 1)

            def split_first():
                split_gate_up(0, lambda m, c: m + c)
                split_down(0, lambda m, c: m + c)
                own.restart()

            groups(dve, steps, between=split_first, last=LAST + 2)

            dve.wait_ge(s["tot_ps"], 1)
            own.link(v.tensor_scalar(tot_i[:], r_tot[:, 0:E + 1], float(UNIT - 1), None, ALU.add))
            own.link(v.tensor_single_scalar(tot_i[:], tot_i[:], 8, ALU.logical_shift_right))
            own.link(v.tensor_scalar(nun[:], tot_i[:], 1.0, None, ALU.max))
            own.put(v.memset(cum[:], 0.0))
            own.wait()
            for e in range(E + 1):
                own.link(v.tensor_tensor(cum[:, e + 1:e + 2], cum[:, e:e + 1], nun[:, e:e + 1], ALU.add))
            own.put(v.tensor_copy(cum_i[:], cum[:]))
            own.put(v.tensor_scalar(step8[:], nun[:, 0:E], -2.0, float(CAP // 128), ALU.mult, ALU.add))
            own.link(v.tensor_tensor(begun[:], iota_f[:, 0:UNITS].unsqueeze(2).to_broadcast([128, UNITS, E + 1]),
                                     cum[:, 1:E + 2].unsqueeze(1).to_broadcast([128, UNITS, E + 1]), ALU.is_ge))
            own.link(v.tensor_tensor(ucol3[:], begun[:, :, 0:E], step8[:].unsqueeze(1).to_broadcast([128, UNITS, E]), ALU.mult))
            own.link(v.tensor_reduce(out=ucol_f[:], in_=ucol3[:], axis=AX.X, op=ALU.add))
            own.link(v.scalar_tensor_tensor(ucol[:], iota_f[:, 0:UNITS], 2.0, ucol_f[:], ALU.mult, ALU.add))
            dve.sem_inc(s["plan_ok"], 1)
            add_table(Counts(dve, LAST + 2))
            dve.wait_ge(s["tab_ok"], B // G)
            own.put(v.tensor_scalar(gidx[:], table[:], 1.0, -1.0, ALU.max, ALU.add))
            own.link(v.tensor_scalar(empty[:], table[:], 0.0, None, ALU.is_equal))
            own.link(v.tensor_tensor(empty[:].rearrange("p (u c) -> p u c", c=2), empty[:].rearrange("p (u c) -> p u c", c=2),
                                     dummy_f[:].unsqueeze(1).to_broadcast([128, TABLE // 2, 2]), ALU.mult))
            own.put(v.scalar_tensor_tensor(sidx[:], table[:], -1.0, empty[:], ALU.add, ALU.add))
            own.wait()
            dve.sem_inc(s["rows_ok"], 1)
            own.put(v.tensor_scalar(uhot[:, :, 0:1], begun[:, :, 0:1], -1.0, 1.0, ALU.mult, ALU.add))
            own.link(v.tensor_tensor(uhot[:, :, 1:E + 1], begun[:, :, 0:E], begun[:, :, 1:E + 1], ALU.subtract))
            own.restart()

            def weights_of(u, u16):
                for i in range(2):
                    dve.wait_ge(hg_in[i], u16)
                own.link(v.tensor_tensor(w9[:], hg[:, :, H:W_FB + 1], uhot[:, bass.ds(u, 1), :].to_broadcast([128, 2, E + 1]), ALU.mult))
                own.put(v.tensor_reduce(out=w_next[:], in_=w9[:], axis=AX.X, op=ALU.add))
                own.link(v.tensor_reduce(out=w_exp[:], in_=w9[:, :, 0:E], axis=AX.X, op=ALU.add))
                v.tensor_tensor(wi_next[:], w_exp[:], hg[:, :, W_INV], ALU.mult).then_inc(s["wi_ok"], 1)

            def next_hT(u1):
                dve.wait_ge(s["gT_hi"], u1)
                v.tensor_tensor(hgT[:, 1, :], bank[0][:], hgT[:, 0, :].bitcast(F32), ALU.subtract).then_inc(s["gT_ok"], 1)

            def unit(g, ft):
                g1 = dve.snap(g + 1)
                g2 = dve.snap(g + 2)

                def product(f):
                    dve.wait_ge(gel_ok[f], g1)
                    v.tensor_tensor(prod[:, f, :], gel[:, f, :], bank[1 + f][:, UNIT:2 * UNIT], ALU.mult).then_inc(prod_ok[f], 1)

                def lower(f):
                    dve.wait_ge(hi_ok[f], g1)
                    v.tensor_tensor(act[:, 1, f, :], prod[:, f, :], act[:, 0, f, :].bitcast(F32), ALU.subtract).then_inc(act_ok[f], 1)

                for f in range(ft):
                    product(f)
                    if f > 0:
                        lower(f - 1)
                    if f == min(2, ft - 1):
                        weights_of(g + 1, dve.snap(g * 16 + 32))
                lower(ft - 1)
                next_hT(g2)
                dve.wait_ge(s["yo_free"], g1)
                dve.wait_ge(s["hw_ok"], g1)
                dve.wait_ge(s["dn_ps"], g2)
                par = dve.snap(g & 1)
                for i in range(2):
                    ins = v.scalar_tensor_tensor(yo[:, i, :], bank[5 + i][:, 0:H], w_now[:, i:i + 1],
                                                 hw[:, bass.ds(par * 2 + i, 1), :].rearrange("p o d -> p (o d)"), ALU.mult, ALU.add)
                    if i == 0:
                        own.put(ins)
                        own.wait()
                ins.then_inc(s["yo_ok"], 1)
                dve.wait_ge(s["yo_ok"], g2)
                own.put(v.tensor_copy(w_now[:], w_next[:]))
                own.restart()

            weights_of(0, 16)
            own.link(v.tensor_copy(w_now[:], w_next[:]))
            own.restart()
            next_hT(1)
            with dve.Fori(0, E // 2) as i2:
                for q in range(2):
                    if q == 0:
                        lo = dve.value_load(cum_i[0:1, bass.ds(i2 * 2, 1)], min_val=0, max_val=UNITS - 3)
                    hi = dve.value_load(cum_i[0:1, bass.ds(i2 * 2 + (q + 1), 1)], min_val=1, max_val=UNITS - 3)
                    count = lambda m, c: dve.snap(i2 * (2 * m) + ((q + 2) * m + c))
                    split_gate_up(1 - q, count)
                    own.restart()
                    with dve.Fori(lo, hi) as g:
                        unit(g, 4)
                    split_down(1 - q, count)
                    lo = hi
            lo = dve.value_load(cum_i[0:1, E:E + 1], min_val=E, max_val=UNITS - 3)
            hi = dve.value_load(cum_i[0:1, E + 1:E + 2], min_val=E + 1, max_val=UNITS - 3)
            with dve.Fori(lo, hi) as g:
                unit(g, 1)

        @block.tensor
        def _(pe):
            t = nc.tensor

            def mm(o, l, r, first, last):
                return t.matmul(o, l, r, start=first, stop=last)

            def transposes(n, k, off):
                slot, p, c = (k + off) % 4, (k + off) % 2, k + off + 1
                n.wait(ctx_in[slot], 32, 32 * ((k + off) // 4 + 1))
                for h, bk_ in enumerate((ps_c0, ps_c1)):
                    n.wait(s[f"c{h}_ok"], 4, c - 1)
                    for i in range(3):
                        last = t.transpose(bk_[:, i * KC:(i + 1) * KC], ctx_sb[:, slot, i, h * 128:(h + 1) * 128], ident[0:KC, 0:KC])
                    last.then_inc(s[f"c{h}_ps"], 1)
                n.wait(s["y_ok"], 4, c)
                n.wait(s["qp_ok"], 4, c - 1)
                for h in range(2):
                    last = t.transpose(ps_q[:, h * S:(h + 1) * S], y_sb[:, p, h * 128:(h + 1) * 128], ident[0:S, 0:S])
                last.then_inc(s["yT_ps"], 1)

            def projections(n, k, off):
                c = k + off + 1
                n.wait(s["c0_ok"], 4, c)
                n.wait(s["c1_ok"], 4, c)
                n.wait(s["kp_ok"], 4, c - 1)
                for h in range(2):
                    last = mm(ps_k[0:QK, 0:C], wk_sb[:, h, :], ctxT[:, h, :], h == 0, h == 1)
                last.then_inc(s["kp_ps"], 1)
                n.wait(s["yT_ok"], 4, c)
                for h in range(2):
                    last = mm(ps_q[0:QK, 2 * S:3 * S], wq_sb[:, h, :], yT[:, h, :], h == 0, h == 1)
                last.then_inc(s["qp_ps"], 1)

            def ranks(n, dst, counts, total, n_e, ok, ps):
                n.wait(s[ok], 1, 0)
                mm(dst, before_r[:], counts[:], True, False)
                for i in range(G - 1):
                    mm(dst[:, i + 1:G, :], ones_r[:, 0:S], counts[:, i, :].unsqueeze(1).to_broadcast([S, G - 1 - i, n_e]), False, False)
                mm(dst, ones_r[:, 0:S], total[:, 0:n_e].unsqueeze(1).to_broadcast([S, G, n_e]), False, True).then_inc(s[ps], 1)

            def table_part(n):
                n.wait(s["hot_ok"], 1, -1)
                n.wait(s["hlo_ok"], 4, -4)
                for i in range(3 * G):
                    last = mm(r_tab, hot_lo[:, i, :], hot_col[:, i, :], i == 0, i == 3 * G - 1)
                last.then_inc(s["tab_ps"], 1)

            def steps(j):
                n = Counts(pe, j)
                tail = isinstance(j, int) and j == LAST + 1
                for k in range(4):
                    if there(j, k, 0):
                        n.wait(s["kp_ok"], 4, k + 1)
                        n.wait(s["qp_ok"], 4, k + 1)
                        n.wait(s["z_ok"], 4, k)
                        for i in range(3):
                            last = mm(ps_s[0:KC, i * S:(i + 1) * S], kpT[:, i * KC:(i + 1) * KC], qpT[:], True, True)
                        last.then_inc(s["s_ps"], 1)
                    if there(j, k, -2):
                        p = k % 2
                        n.wait(s["h_ok"], 4, k - 1)
                        n.wait(s["av_ok"], 4, k if there(j, k, -1) else k - 1)
                        for h in range(2):
                            last = t.transpose(ps_v[:, (2 + h) * S:(3 + h) * S], h_sb[:, p, h * 128:(h + 1) * 128], ident[0:S, 0:S])
                        last.then_inc(s["hT_ps"], 1)
                    if there(j, k, -1):
                        p = (k - 1) % 2
                        n.wait(s["av_ok"], 4, k)
                        n.wait(s["x1_ok"], 4, k - 1)
                        for h in range(2):
                            mm(ps_o[0:S, 0:H], avT[:, h, :], wv_sb[:, h, :], h == 0, False)
                        n.wait(s["zs_ok"], 4, k)
                        mm(ps_o[0:S, 0:H], zs[:], bv_sb[:], False, True).then_inc(s["o_ps"], 1)
                    if there(j, k, 0):
                        slot = k % 4
                        n.wait(s["z_ok"], 4, k + 1)
                        n.wait(s["hT_ok"], 4, k - 1)
                        for h in range(2):
                            for i in range(3):
                                last = mm(ps_v[:, h * S:(h + 1) * S], ctx_sb[:, slot, i, h * 128:(h + 1) * 128],
                                          z_sb[:, k % 2, i, :], i == 0, i == 2)
                        last.then_inc(s["av_ps"], 1)
                    if k > 0 and group_there(j, -2 if k == 1 else -1):
                        n.wait(s["lg_ok"], 4, min(k - 2, B - 4 * j) if isinstance(j, int) else k - 2)
                    if k == 1 and group_there(j, -2) and not tail:
                        table_part(n)
                    if k == 2 and group_there(j, -1):
                        ranks(n, r_pos, cnt, carry, E, "top_ok", "pos_ps")
                    if k == 3 and group_there(j, -1):
                        ranks(n, r_pos2, cnt2, carry2, E2, "cnt2_ok", "pos2_ps")
                        if tail:
                            pe.wait_ge(s["carried"], 1)
                            mm(r_tot[:, 0:E + 1], ones[0:S, :], carry2[:, 0:E + 1].bitcast(F32), True, True).then_inc(s["tot_ps"], 1)
                    if there(j, k, 1):
                        projections(n, k, 1)
                    if there(j, k, -2):
                        n.wait(s["hT_ok"], 4, k - 1)
                        n.wait(s["lg_ok"], 4, k - 2)
                        if k == 1 and group_there(j, -2) and not tail:
                            n.wait(s["tab_ok"], 1, -1)
                        if k == 2 and group_there(j, -1):
                            n.wait(s["pos_rd"], 1, 0)
                        if k == 3 and group_there(j, -1):
                            n.wait(s["pos2_rd"], 1, 0)
                        for h in range(2):
                            last = mm(r_logit, hT[:, h, :], wr_sb[:, h, :], h == 0, h == 1)
                        last.then_inc(s["lg_ps"], 1)
                    if tail and k == 1:
                        pe.wait_ge(s["lg_ok"], B)
                        table_part(n)
                        pe.wait_ge(s["tab_ok"], LAST)
                    if there(j, k, 2):
                        transposes(n, k, 2)

            pe.wait_ge(s["c_dve"], 1)
            pe.wait_ge(s["c_tanh"], 3)
            n = Counts(pe, 0)
            transposes(n, -2, 2)
            projections(n, -1, 1)
            transposes(n, -1, 2)
            groups(pe, steps)
            pe.wait_ge(s["plan_ok"], 1)

            def next_hT(u16):
                for i in range(2):
                    pe.wait_ge(hg_in[i], u16)
                    for h in range(2):
                        last = t.transpose(bank[0][:, h * UNIT + i * 128:h * UNIT + (i + 1) * 128],
                                           hg[:, i, h * 128:(h + 1) * 128], ident[:])
                last.then_inc(s["gT_ps"], 1)

            def unit(g, e1, ft, q):
                g1 = pe.snap(g + 1)
                parts = ((0, 0), (0, 1), (1, 0))
                pe.wait_ge(s["gT_ok"], g1)
                for f in range(ft):
                    for i, w in enumerate((wg_sb[q], wu_sb[q])):
                        for h in range(2):
                            for a, b in parts:
                                last = mm(bank[1 + f][:, i * UNIT:(i + 1) * UNIT], w[:, a, h, f * 128:(f + 1) * 128], hgT[:, b, h * UNIT:(h + 1) * UNIT],
                                          h == 0 and (a, b) == (0, 0), h == 1 and (a, b) == (1, 0))
                    last.then_inc(gu_ps[f], 1)
                pe.wait_ge(s["yo_ok"], g1)
                pe.wait_ge(s["wd_split"], e1)
                for f in range(ft):
                    pe.wait_ge(act_ok[f], g1)
                    for i in range(2):
                        for a, b in parts:
                            last = mm(bank[5 + i][:, 0:H], act[:, a, f, i * 128:(i + 1) * 128], wd_sb[q][:, b, f, :],
                                      f == 0 and (a, b) == (0, 0), f == ft - 1 and (a, b) == (1, 0))
                    if f == ft - 1:
                        last.then_inc(s["dn_ps"], 1)
                    if f == 0:
                        next_hT(pe.snap(g * 16 + 32))

            next_hT(16)
            with pe.Fori(0, E // 2) as i2:
                for q in range(2):
                    if q == 0:
                        lo = pe.value_load(cum_i[0:1, bass.ds(i2 * 2, 1)], min_val=0, max_val=UNITS - 3)
                    hi = pe.value_load(cum_i[0:1, bass.ds(i2 * 2 + (q + 1), 1)], min_val=1, max_val=UNITS - 3)
                    e1 = pe.snap(i2 * 2 + (q + 1))
                    pe.wait_ge(s["gu_split"], e1)
                    settle(pe, s["settled"])
                    with pe.Fori(lo, hi) as g:
                        unit(g, e1, 4, q)
                    lo = hi
            lo = pe.value_load(cum_i[0:1, E:E + 1], min_val=E, max_val=UNITS - 3)
            hi = pe.value_load(cum_i[0:1, E + 1:E + 2], min_val=E + 1, max_val=UNITS - 3)
            pe.wait_ge(s["gu_split"], E + 1)
            settle(pe, s["settled"])
            with pe.Fori(lo, hi) as g:
                unit(g, E + 1, 1, 0)


def kernel(**inputs):
    import numpy as _np
    import concourse.bacc as _bacc
    from concourse.bass_utils import run_bass_kernel_spmd as _run

    a = {k: _np.asarray(v) for k, v in inputs.items()}
    norms = _np.concatenate([a["L0_ffn_norm_w"], a["L0_ffn_f_norm"][None]], 0)
    arrays = {
        "x": a["x"].reshape(N, H),
        "ctx_rows": a["ctx_1024"].reshape(B * C, H),
        "g2": _np.concatenate([a["g_xattn"], a["g_ffn"]]),
        "wqT": a["L0_xattn_Wq"].T, "bq": a["L0_xattn_bq"],
        "wkT": a["L0_xattn_Wk"].T, "bk": a["L0_xattn_bk"],
        "wvT": a["L0_xattn_Wv"].T, "bv": a["L0_xattn_bv"],
        "wr": a["L0_ffn_Wr"],
        "norms": norms.reshape(E + 1, 2, 128).transpose(2, 0, 1),
        "wg": a["L0_ffn_Wg"], "wu": a["L0_ffn_Wu"], "wd": a["L0_ffn_Wd"],
        "fwg": a["L0_ffn_fWg"], "fwu": a["L0_ffn_fWu"], "fwd": a["L0_ffn_fWd"],
    }
    arrays = {k: _np.ascontiguousarray(v) for k, v in arrays.items()}
    nc = _bacc.Bacc("TRN2", target_bir_lowering=False, num_devices=1)
    args = [nc.dram_tensor(k, v.shape, mybir.dt.from_np(v.dtype), kind="ExternalInput").ap() for k, v in arrays.items()]
    out = nc.dram_tensor("out", [N + DUMMY, H], F32, kind="ExternalOutput").ap()
    build(nc, *args, out)
    r = _run(nc, [arrays], core_ids=[0])
    return r.results[0]["out"][:N].reshape(B, S, H)
```

```python
import numpy as np
import concourse.bass as bass
from concourse import mybir
from contextlib import ExitStack

F32 = mybir.dt.float32
F32R = mybir.dt.float32r
I32 = mybir.dt.int32
ALU = mybir.AluOpType
ACT = mybir.ActivationFunctionType
AX = mybir.AxisListType

B, S, H, C = 32, 112, 256, 375
KC = C // 3
QK = 64
E, F, FB = 8, 512, 128
E2 = E + 2
CAP = 1024
N = B * S
G = 4
UNIT = 256
COLS = E * CAP // 128
FCOLS = 32
TABLE = COLS + FCOLS
UNITS = 40
PAY = 272
W_FB, W_INV, W_NONE = H + E, H + E + 1, H + E + 2
DUMMY = UNIT
PARTS = ((0, 0), (0, 1), (1, 0))
LN_EPS, RMS_EPS = 1e-5, 1e-6


class Chain:

    def __init__(self, engine, sem):
        self.engine, self.sem, self.n = engine, sem, 0

    def put(self, ins):
        ins.then_inc(self.sem, 1)
        self.n += 1

    def link(self, ins):
        self.put(ins)
        self.engine.wait_ge(self.sem, self.n)

    def wait(self):
        self.engine.wait_ge(self.sem, self.n)

    def restart(self):
        if self.n:
            self.engine.wait_ge(self.sem, self.n)
            self.engine.sem_clear(self.sem)
            self.n = 0


def settle(engine, sem):
    engine.sem_inc(sem, 1)


class Counts:

    def __init__(self, engine, j):
        self.engine, self.j, self.kept = engine, j, {}

    def __call__(self, a, c):
        if isinstance(self.j, int):
            return a * self.j + c
        if (a, c) not in self.kept:
            self.kept[a, c] = self.engine.snap(self.j * a + c)
        return self.kept[a, c]

    def wait(self, sem, a, c):
        v = self(a, c)
        if not isinstance(v, int) or v > 0:
            self.engine.wait_ge(sem, v)


def build(nc, x, ctx_rows, g2, wqT, bq, wkT, bk, wvT, bv, wr, norms, wg, wu, wd, fwg, fwu, fwd, out):
    stack = ExitStack()
    with stack:
        def sb(name, shape, dt=F32):
            return stack.enter_context(nc.sbuf_tensor(name, shape, dt))

        def sem(name):
            return stack.enter_context(nc.semaphore(name))

        payload = nc.dram_tensor("payload", [N, PAY], F32).ap()

        ident = sb("ident", [128, 128])
        before = sb("before", [S, S])
        ones = sb("ones", [128, 128])
        before_r = sb("before_r", [S, S], F32R)
        ones_r = sb("ones_r", [S, 128], F32R)
        iota_i = sb("iota_i", [128, 128], I32)
        iota_f = sb("iota_f", [128, 128])
        rev8 = sb("rev8", [S, E])
        ids = sb("ids", [S, 2, G])
        ids_i = sb("ids_i", [S, G], I32)
        dummy_i = sb("dummy_i", [128, 2], I32)
        dummy_f = sb("dummy_f", [128, 2])
        zeros = sb("zeros", [128, 2 * H])
        exph = sb("exph", [S, 1])
        gate_copy = sb("gate_copy", [128, 2])
        gates = sb("gates", [128, 2])
        tg = sb("tg", [128, 2])
        wq_sb = sb("wq_sb", [128, 2, QK])
        wk_sb = sb("wk_sb", [128, 2, QK])
        wv_sb = sb("wv_sb", [128, 2, H])
        wv_split = sb("wv_split", [128, 2, 2, H], F32R)
        wr_sb = sb("wr_sb", [128, 2, E])
        bq_sb = sb("bq_sb", [QK, 1])
        bk_sb = sb("bk_sb", [QK, 1])
        bv_sb = sb("bv_sb", [KC, H])

        x_sb = sb("x_sb", [S, 4, H])
        ctx_sb = sb("ctx_sb", [KC, 4, 3, H])
        stat1 = sb("stat1", [S, 2, 6])
        mv1 = sb("mv1", [S, 2, 2])
        arg1 = sb("arg1", [S, 2, 1])
        rs1 = sb("rs1", [S, 2, 1])
        y_sb = sb("y_sb", [S, 2, H])
        yT = sb("yT", [128, 2, S])
        ctxT = sb("ctxT", [128, 2, C])
        kpT = sb("kpT", [QK, C])
        qpT = sb("qpT", [QK, S])
        z_sb = sb("z_sb", [KC, 2, 3, S])
        avT = sb("avT", [128, 2, 2, S], F32R)
        x1 = sb("x1", [S, 2, H])
        stat2 = sb("stat2", [S, 2, 6])
        mv2 = sb("mv2", [S, 2, 2])
        arg3 = sb("arg3", [S, 2, 3])
        rs3 = sb("rs3", [S, 2, 3])
        ab = sb("ab", [S, 2, 3])
        h_sb = sb("h_sb", [S, 2, H])
        zs = sb("zs", [KC, S])
        inv_t = sb("inv_t", [S, 2, 1])
        base = sb("base", [S, 2, H])
        hT = sb("hT", [128, 2, S])
        logit = sb("logit", [S, G, E])
        inv_g = sb("inv_g", [S, G])
        m12 = sb("m12", [S, 2, G])
        eq = sb("eq", [S, G, E])
        rest = sb("rest", [S, G, E])
        mi3 = sb("mi3", [S, G, 3])
        oh = sb("oh", [S, G, 2, E])
        cnt = sb("cnt", [S, G, E], F32R)
        cnt2 = sb("cnt2", [S, G, E2], F32R)
        carry = sb("carry", [S, E2], F32R)
        carry2 = sb("carry2", [S, E2], F32R)
        csum = sb("csum", [S, E2])
        expo = sb("expo", [S, G * E])
        ex = sb("ex", [S, G * E])
        sg = sb("sg", [S, 2, G * E])
        den = sb("den", [S, 2, G])
        wnum = sb("wnum", [S, G, E])
        extra = sb("extra", [S, G, PAY - H])
        pm = sb("pm", [S, G, 2, E])
        pos = sb("pos", [S, G, 2])
        drop = sb("drop", [S, G, 2])
        ovf = sb("ovf", [S, G])
        keep = sb("keep", [S, G])
        cpos = sb("cpos", [S, G, 3])
        pen = sb("pen", [S, G, 3])
        slot_i = sb("slot_i", [S, G * 3], I32)
        lc_i = sb("lc_i", [S, 2, G * 3], I32)
        lc = sb("lc", [S, 2, G * 3])
        off = sb("off", [S, G * 3, 128])
        hot_lo = sb("hot_lo", [S, G * 3, 128], F32R)
        hot_col = sb("hot_col", [S, G * 3, TABLE], F32R)
        table = sb("table", [128, TABLE])
        gidx = sb("gidx", [128, TABLE], I32)
        empty = sb("empty", [128, TABLE])
        sidx = sb("sidx", [128, TABLE], I32)
        tot_i = sb("tot_i", [128, E + 1], I32)
        nun = sb("nun", [128, E + 1])
        cum = sb("cum", [128, 2, E + 2])
        cum_i = sb("cum_i", [128, E + 2], I32)
        step8 = sb("step8", [128, E])
        begun = sb("begun", [128, UNITS, E + 1])
        ucol3 = sb("ucol3", [128, UNITS, E])
        ucol_f = sb("ucol_f", [128, UNITS])
        ucol = sb("ucol", [128, UNITS], I32)
        uhot = sb("uhot", [128, UNITS, E + 1])
        raw_g = sb("raw_g", [128, 2, F])
        raw_u = sb("raw_u", [128, 2, F])
        raw_d = sb("raw_d", [128, 4, H])
        raw_n = sb("raw_n", [128, 2])
        wg_sb = [sb(f"wg_sb{q}", [128, 2, 2, F], F32R) for q in range(2)]
        wu_sb = [sb(f"wu_sb{q}", [128, 2, 2, F], F32R) for q in range(2)]
        wd_sb = [sb(f"wd_sb{q}", [128, 2, 4, H], F32R) for q in range(2)]
        gidx_now = sb("gidx_now", [128, 2], I32)
        sidx_now = sb("sidx_now", [128, 2], I32)
        sidx_u = sb("sidx_u", [128, UNITS, 2], I32)
        hg = sb("hg", [128, 2, PAY])
        w9 = sb("w9", [128, 2, E + 1])
        w_next = sb("w_next", [128, 2])
        w_now = sb("w_now", [128, 2])
        w_exp = sb("w_exp", [128, 2])
        wi_next = sb("wi_next", [128, 2])
        hw = sb("hw", [128, 4, H])
        hgT = sb("hgT", [128, 2, 2 * UNIT], F32R)
        gel = sb("gel", [128, 4, UNIT])
        prod = sb("prod", [128, 4, UNIT])
        act = sb("act", [128, 2, 4, UNIT], F32R)
        yo = sb("yo", [128, 2, H])

        bank = [stack.enter_context(nc.psum_tensor(f"bank{i}", [128, 512], F32)) for i in range(8)]
        ps_c0, ps_c1 = bank[0], bank[1]
        ps_q, ps_k, ps_s, ps_v, ps_o, ps_r = bank[2:8]
        r_logit = ps_r[0:S, 0:E]
        r_pos = ps_r[0:S, 32:32 + G * E].rearrange("p (g e) -> p g e", e=E)
        r_pos2 = ps_r[0:S, 64:64 + G * E2].rearrange("p (g e) -> p g e", e=E2)
        r_tab = ps_r[:, 128:128 + TABLE]
        r_tot = ps_s[:, 0:E + 2]

        names = ("proj_in const_in c_gp c_dve c_tanh dve_own act_own pool_own "
                 "st1 rs1_ok y_ok yT_ps c0_ps c1_ps yT_ok c0_ok c1_ok kp_ps qp_ps kp_ok qp_ok s_ps z_ok "
                 "av_ps av_hi av_ok wv_hi wv_ok o_ps x1_ok st2 rs3_ok h_ok base_ok zs_ok inv_ok inv_rd hT_ps hT_ok lg_ps lg_ok "
                 "top_ok ex_ok pos_ps pos_rd cnt2_ok pos2_ps pos2_rd wd_ok lc_ok hlo_ok hot_ok carried tab_ps tab_ok ext_out "
                 "tot_ps plan_ok rows_ok fill_out raw_gu raw_dn gu_hi gu_split wd_hi wd_split gT_ps gT_hi gT_ok wi_ok hw_ok yo_ok yo_free "
                 "dn_ps settled").split()
        s = {n: sem(n) for n in names}
        x_in = [sem(f"x_in{i}") for i in range(4)]
        ctx_in = [sem(f"ctx_in{i}") for i in range(4)]
        h_out = [sem(f"h_out{i}") for i in range(2)]
        base_out = [sem(f"base_out{i}") for i in range(2)]
        hg_in = [sem(f"hg_in{i}") for i in range(2)]
        added = [sem(f"added{i}") for i in range(2)]
        gu_ps = [sem(f"gu_ps{i}") for i in range(4)]
        gel_ok = [sem(f"gel_ok{i}") for i in range(4)]
        prod_ok = [sem(f"prod_ok{i}") for i in range(4)]
        hi_ok = [sem(f"hi_ok{i}") for i in range(4)]
        act_ok = [sem(f"act_ok{i}") for i in range(4)]

        LAST = B // G - 1
        N_CONST = 4

        def groups(engine, body, before_tail=None, first=0, loop=(2, 7), last=LAST + 3):
            for j in range(first, loop[0]):
                body(j)
            with engine.Fori(loop[0], loop[1]) as j:
                body(j)
            if before_tail:
                before_tail()
            for j in range(loop[1], last):
                body(j)

        def there(j, k, off):
            return not isinstance(j, int) or 0 <= G * j + k + off < B

        def group_there(j, off):
            return not isinstance(j, int) or 0 <= j + off <= LAST

        block = stack.enter_context(nc.Block())

        @block.sync
        def _(sp):
            def load_x(row, slot):
                sp.dma_start(x_sb[:, slot, :], x[bass.ds(row, S), :]).then_inc(x_in[slot], 16)

            def load_ctx(ctx_row, slot):
                sp.dma_start(ctx_sb[0:S, slot],
                             ctx_rows[bass.ds(ctx_row, 3 * S), :].rearrange("(p c) d -> p c d", c=3)).then_inc(ctx_in[slot], 16)
                sp.dma_start(ctx_sb[S:KC, slot],
                             ctx_rows[bass.ds(ctx_row + 3 * S, C - 3 * S), :].rearrange("(p c) d -> p c d", c=3)).then_inc(ctx_in[slot], 16)

            load_x(0, 0)
            load_ctx(0, 0)
            sp.dma_start(wk_sb[:], wkT.rearrange("(k p) d -> p k d", p=128)).then_inc(s["proj_in"], 16)
            sp.dma_start(wq_sb[:], wqT.rearrange("(k p) d -> p k d", p=128)).then_inc(s["proj_in"], 16)
            with nc.allow_non_contiguous_dma(reason="small constants"):
                sp.dma_start(bq_sb[:], bq.rearrange("(p o) -> p o", o=1)).then_inc(s["proj_in"], 16)
                sp.dma_start(bk_sb[:], bk.rearrange("(p o) -> p o", o=1)).then_inc(s["proj_in"], 16)
            load_x(S, 1)
            load_ctx(C, 1)
            sp.dma_start(wv_sb[:], wvT.rearrange("(k p) d -> p k d", p=128)).then_inc(s["const_in"], 16)
            with nc.allow_non_contiguous_dma(reason="small constants"):
                sp.dma_start(gates[:], g2.rearrange("(o a) -> o a", o=1).to_broadcast([128, 2])).then_inc(s["const_in"], 16)
                sp.dma_start(bv_sb[:], bv.rearrange("(o a) -> o a", o=1).to_broadcast([KC, H])).then_inc(s["const_in"], 16)
            sp.dma_start(wr_sb[:], wr.rearrange("(k p) d -> p k d", p=128)).then_inc(s["const_in"], 16)
            load_x(2 * S, 2)
            load_ctx(2 * C, 2)
            sp.wait_ge(s["c_gp"], 1)
            sp.dma_start(out[N:N + DUMMY, :].rearrange("(p c) d -> p (c d)", c=2), zeros[:]).then_inc(s["fill_out"], 16)

            def load_gate_up(src_g, src_u, src_n, width):
                sp.dma_start(raw_g[:, :, 0:width], src_g).then_inc(s["raw_gu"], 16)
                sp.dma_start(raw_u[:, :, 0:width], src_u).then_inc(s["raw_gu"], 16)
                with nc.allow_non_contiguous_dma(reason="8 B of a norm's weights per row"):
                    sp.dma_start(raw_n[:], src_n).then_inc(s["raw_gu"], 16)

            def expert_gate_up(e):
                load_gate_up(wg[bass.ds(e, 1)].rearrange("o (k p) f -> p (o k) f", p=128),
                             wu[bass.ds(e, 1)].rearrange("o (k p) f -> p (o k) f", p=128),
                             norms[:, bass.ds(e, 1), :].rearrange("p o k -> p (o k)"), F)

            def expert_down(e):
                sp.dma_start(raw_d[:], wd[bass.ds(e, 1)].rearrange("o (k p) d -> p (o k) d", p=128)).then_inc(s["raw_dn"], 16)

            def weights(e):
                if not isinstance(e, int) or e > 0:
                    sp.wait_ge(s["gu_split"], 4 * e if isinstance(e, int) else sp.snap(e * 4))
                expert_gate_up(e)
                if not isinstance(e, int) or e > 0:
                    sp.wait_ge(s["wd_split"], e)
                expert_down(e)

            def steps(j):
                n = Counts(sp, j)
                for k in range(4):
                    if isinstance(j, int) and (j, k) == (0, 2):
                        weights(0)
                    if k == 0 and group_there(j, -2):
                        n.wait(s["wd_ok"], 1, -1)
                        with nc.allow_non_contiguous_dma(reason="64 B of weights per token"):
                            sp.dma_start(payload[bass.ds(G * S * (j - 2), G * S), H:PAY].rearrange("(g p) c -> p g c", g=G),
                                         extra[:]).then_inc(s["ext_out"], 16)
                    if there(j, k, 3):
                        n.wait(s["av_ps"], 4, k)
                        load_ctx(G * C * j + (k + 3) * C, (k + 3) % 4)
                        n.wait(s["x1_ok"], 4, k)
                        load_x(G * S * j + (k + 3) * S, (k + 3) % 4)
                    if there(j, k, -1):
                        row = G * S * j + (k - 1) * S
                        p = (k - 1) % 2
                        n.wait(s["h_ok"], 4, k)
                        sp.dma_start(payload[bass.ds(row, S), 0:H], h_sb[:, p, :]).then_inc(h_out[p], 16)
                        n.wait(s["base_ok"], 4, k)
                        sp.dma_start(out[bass.ds(row, S), :], base[:, p, :]).then_inc(base_out[p], 16)

            groups(sp, steps, before_tail=lambda: weights(1))
            with sp.Fori(2, E) as e:
                weights(e)
            sp.wait_ge(s["gu_split"], 4 * E)
            load_gate_up(fwg.rearrange("(k p) f -> p k f", p=128), fwu.rearrange("(k p) f -> p k f", p=128), norms[:, E, :], FB)
            sp.wait_ge(s["wd_split"], E)
            sp.dma_start(raw_d[:, 0, :], fwd).then_inc(s["raw_dn"], 16)
            for p in range(2):
                sp.wait_ge(base_out[p], 16 * B // 2)

        @block.gpsimd
        def _(pool):
            own = Chain(pool, s["pool_own"])
            gp = nc.gpsimd
            own.put(gp.memset(ones[:], 1.0))
            own.put(gp.iota(iota_i[:], [[1, 128]], 0, 0))
            own.put(gp.iota(ids_i[:], [[S, G]], 1 - G * S, 1))
            own.put(gp.iota(dummy_i[:], [[128, 2]], N + 1, 1))
            own.put(gp.memset(exph[:], -0.5))
            own.put(gp.memset(mi3[:], 0.0))
            own.put(gp.memset(extra[:], 0.0))
            own.put(gp.memset(table[:], 0.0))
            own.put(gp.memset(cnt2[:].bitcast(F32), 0.0))
            own.put(gp.memset(carry[:].bitcast(F32), 0.0))
            own.put(gp.memset(carry2[:].bitcast(F32), 0.0))
            own.link(gp.memset(zeros[:], 0.0))
            own.put(gp.affine_select(out=ident[:], in_=ones[:], compare_op=ALU.is_equal, fill=0.0, base=0,
                                     pattern=[[-1, 128]], channel_multiplier=1))
            own.link(gp.affine_select(out=before[:], in_=ones[0:S, 0:S], compare_op=ALU.is_gt, fill=0.0, base=0,
                                      pattern=[[1, S]], channel_multiplier=-1))
            pool.sem_inc(s["c_gp"], 1)
            pool.sem_inc(s["yo_free"], 1)
            pool.sem_inc(s["dn_ps"], 1)

            def steps(j):
                n = Counts(pool, j)
                for k in range(4):
                    if there(j, k, 2):
                        p = k % 2
                        n.wait(s["st1"], 4, k + 3)
                        settle(pool, s["settled"])
                        own.link(gp.tensor_scalar(arg1[:, p, :], mv1[:, p, 1:2], 1.0, LN_EPS, ALU.mult, ALU.add))
                        gp.tensor_tensor(rs1[:, p, :], arg1[:, p, :], exph[:], ALU.pow).then_inc(s["rs1_ok"], 1)
                    if there(j, k, 0):
                        n.wait(s["z_ok"], 4, k + 1)
                        n.wait(s["o_ps"], 4, k)
                        own.link(gp.tensor_tensor(zs[:], z_sb[:, k % 2, 0, :], z_sb[:, k % 2, 1, :], ALU.add))
                        gp.tensor_tensor(zs[:], zs[:], z_sb[:, k % 2, 2, :], ALU.add).then_inc(s["zs_ok"], 1)
                    if isinstance(j, int) and (j, k) == (0, 1):
                        pool.wait_ge(s["c_tanh"], 1)
                    if there(j, k, -1):
                        p = (k - 1) % 2
                        n.wait(s["st2"], 4, k)
                        settle(pool, s["settled"])
                        own.link(gp.tensor_scalar(arg3[:, p, 0:1], mv2[:, p, 1:2], 1.0 + RMS_EPS, RMS_EPS * LN_EPS, ALU.mult, ALU.add))
                        gp.tensor_tensor(rs3[:, p, 0:1], arg3[:, p, 0:1], exph[:], ALU.pow).then_inc(s["rs3_ok"], 1)
                        own.link(gp.tensor_scalar(arg3[:, p, 1:2], mv2[:, p, 1:2], 1.0, LN_EPS, ALU.mult, ALU.add))
                        own.link(gp.tensor_tensor(rs3[:, p, 1:2], arg3[:, p, 1:2], exph[:], ALU.pow))
                        n.wait(s["rs3_ok"], 4, k)
                        own.put(gp.tensor_tensor(rs3[:, p, 2:3], arg3[:, p, 0:1], rs3[:, p, 0:1], ALU.mult))
                        own.put(gp.tensor_tensor(ab[:, p, 2:3], mv2[:, p, 0:1], rs3[:, p, 1:2], ALU.mult))
                        own.link(gp.tensor_scalar(ab[:, p, 0:1], rs3[:, p, 1:2], tg[0:S, 1:2], 1.0, ALU.mult, ALU.add))
                        own.link(gp.tensor_scalar(ab[:, p, 1:2], ab[:, p, 2:3], tg[0:S, 1:2], -1.0, ALU.mult, ALU.mult))
                        n.wait(s["inv_rd"], 4, k - 2)
                        gp.tensor_tensor(inv_t[:, p, :], rs3[:, p, 1:2], rs3[:, p, 2:3], ALU.mult).then_inc(s["inv_ok"], 1)
                        n.wait(base_out[p], 32, 16 * ((k - 1) // 2))
                        settle(pool, s["settled"])
                        gp.tensor_scalar(base[:, p, :], x1[:, p, :], ab[:, p, 0:1], ab[:, p, 1:2], ALU.mult, ALU.add).then_inc(s["base_ok"], 1)
                own.restart()

            for t in range(2):
                pool.wait_ge(s["st1"], t + 1)
                own.link(gp.tensor_scalar(arg1[:, t, :], mv1[:, t, 1:2], 1.0, LN_EPS, ALU.mult, ALU.add))
                gp.tensor_tensor(rs1[:, t, :], arg1[:, t, :], exph[:], ALU.pow).then_inc(s["rs1_ok"], 1)
            own.restart()
            groups(pool, steps)

            pool.wait_ge(s["rows_ok"], 1)
            pool.wait_ge(s["ext_out"], 16 * (B // G))
            pool.wait_ge(s["fill_out"], 16)
            for p in range(2):
                pool.wait_ge(h_out[p], 16 * B // 2)
                pool.wait_ge(base_out[p], 16 * B // 2)

            def gather(u, col):
                own.link(gp.tensor_copy(gidx_now[:], gidx[:, col:col + 2] if isinstance(col, int) else gidx[:, bass.ds(col, 2)]))
                for i in range(2):
                    gp.indirect_dma_start(out=hg[:, i, :], out_offset=None, in_=payload,
                                          in_offset=bass.IndirectOffsetOnAxis(ap=gidx_now[:, i:i + 1], axis=0)).then_inc(hg_in[i], 16)
                own.put(gp.tensor_copy(sidx_u[:, bass.ds(u, 1), :].rearrange("p o c -> p (o c)"), sidx[:, bass.ds(col, 2)]))

            def ahead(u, parity):
                col = pool.value_load(ucol[0:1, bass.ds(u + 1, 1)], min_val=0, max_val=TABLE - 2)
                pool.wait_ge(s["wi_ok"], pool.snap(u + 1))
                settle(pool, s["settled"])
                gp.tensor_tensor(hw[:, bass.ds(parity * 2, 2), :], hg[:, :, 0:H], wi_next[:].unsqueeze(2).to_broadcast([128, 2, H]),
                                 ALU.mult).then_inc(s["hw_ok"], 1)
                pool.wait_ge(s["hw_ok"], pool.snap(u + 1))
                pool.wait_ge(s["gT_ps"], pool.snap(u + 1))
                gather(u + 1, col)

            def scatter(u):
                pool.wait_ge(s["yo_ok"], pool.snap(u * 2 + 4))
                own.link(gp.tensor_copy(sidx_now[:], sidx_u[:, bass.ds(u, 1), :].rearrange("p o c -> p (o c)")))
                for i in range(2):
                    gp.indirect_dma_start(out=out, out_offset=bass.IndirectOffsetOnAxis(ap=sidx_now[:, i:i + 1], axis=0),
                                          in_=yo[:, i, :], in_offset=None, compute_op=ALU.add).then_inc(added[i], 16)

            gather(0, 0)
            n_units = pool.value_load(cum_i[0:1, E + 1:E + 2], min_val=E + 1, max_val=UNITS - 3)
            own.restart()
            ahead(0, 0)
            ahead(1, 1)
            own.restart()
            with pool.Fori(1, n_units) as g:
                scatter(g - 1)
                ahead(g + 1, pool.snap((g + 1) & 1))
                g16 = pool.snap(g * 16)
                for i in range(2):
                    pool.wait_ge(added[i], g16)
                pool.sem_inc(s["yo_free"], 1)
                own.restart()
            scatter(n_units - 1)
            for i in range(2):
                pool.wait_ge(added[i], pool.snap(n_units * 16))
                pool.wait_ge(hg_in[i], pool.snap(n_units * 16 + 32))

        @block.scalar
        def _(act_e):
            sc = nc.scalar
            def head(n, k, off):
                c = k + off + 1
                n.wait(s["c0_ps"], 4, c)
                sc.activation(ctxT[:, 0, :], ps_c0[:, 0:C], ACT.Copy).then_inc(s["c0_ok"], 1)
                n.wait(s["c1_ps"], 4, c)
                sc.activation(ctxT[:, 1, :], ps_c1[:, 0:C], ACT.Copy).then_inc(s["c1_ok"], 1)
                n.wait(s["yT_ps"], 4, c)
                sc.activation(yT[:], ps_q[:, 0:2 * S].rearrange("p (k q) -> p k q", k=2), ACT.Copy).then_inc(s["yT_ok"], 1)

            def proj(n, k, off):
                c = k + off + 1
                n.wait(s["kp_ps"], 4, c)
                sc.activation(kpT[:], ps_k[0:QK, 0:C], ACT.Identity, bias=bk_sb[:]).then_inc(s["kp_ok"], 1)
                n.wait(s["qp_ps"], 4, c)
                sc.activation(qpT[:], ps_q[0:QK, 2 * S:3 * S], ACT.Identity, bias=bq_sb[:]).then_inc(s["qp_ok"], 1)

            def hot_rows(n, part):
                size = 3
                n.wait(s["lc_ok"], 1, -1)
                for i in range(part * size, (part + 1) * size):
                    last = sc.activation(off[:, i, :], iota_f[0:S, :], ACT.Abs, scale=-1.0, bias=lc[:, 0, i:i + 1])
                last.then_inc(s["act_own"], 1)
                n.wait(s["act_own"], 4, part - 7)
                sc.activation(hot_lo[:, part * size:(part + 1) * size, :], off[:, part * size:(part + 1) * size, :],
                              ACT.Relu, scale=ids[:, 1, part:part + 1], bias=ids[:, 0, part:part + 1]).then_inc(s["hlo_ok"], 1)

            def split_gate_up(q, count, parts=range(4)):
                act_e.wait_ge(s["raw_gu"], count(48))
                for i in parts:
                    k, w, raw = ((0, wg_sb[q], raw_g), (0, wu_sb[q], raw_u), (1, wg_sb[q], raw_g), (1, wu_sb[q], raw_u))[i]
                    sc.activation(w[:, 0, k, :], raw[:, k, :], ACT.Copy, scale=raw_n[:, k:k + 1]).then_inc(s["gu_hi"], 1)

            def split_down(q, count):
                act_e.wait_ge(s["raw_dn"], count(16))
                sc.activation(wd_sb[q][:, 0], raw_d[:], ACT.Copy).then_inc(s["wd_hi"], 1)

            def steps(j):
                n = Counts(act_e, j)
                for k in range(4):
                    if there(j, k, 0):
                        n.wait(s["s_ps"], 4, k + 1)
                        n.wait(s["zs_ok"], 4, k - 1)
                        sc.activation(z_sb[:, k % 2], ps_s[0:KC, 0:3 * S].rearrange("p (c q) -> p c q", c=3),
                                      ACT.Sigmoid, scale=1.0 / float(np.sqrt(QK))).then_inc(s["z_ok"], 1)
                    if there(j, k, -2):
                        n.wait(s["hT_ps"], 4, k - 1)
                        sc.activation(hT[:], ps_v[:, 2 * S:4 * S].rearrange("p (k q) -> p k q", k=2), ACT.Copy).then_inc(s["hT_ok"], 1)
                    if k == 2 and group_there(j, -1):
                        n.wait(s["top_ok"], 1, 0)
                        sc.activation(sg[:, 0, :], expo[:], ACT.Sigmoid)
                        sc.activation(sg[:, 1, :], expo[:], ACT.Sigmoid, scale=-1.0).then_inc(s["ex_ok"], 1)
                    if isinstance(j, int) and (j, k) == (0, 0):
                        act_e.wait_ge(s["const_in"], 16 * N_CONST)
                        sc.activation(tg[:], gates[:], ACT.Tanh).then_inc(s["c_tanh"], 1)
                        act_e.wait_ge(s["c_tanh"], 1)
                        sc.activation(wv_sb[:], wv_sb[:], ACT.Copy, scale=tg[:, 0:1]).then_inc(s["c_tanh"], 1)
                        sc.activation(bv_sb[:], bv_sb[:], ACT.Copy, scale=tg[0:KC, 0:1]).then_inc(s["c_tanh"], 1)
                        act_e.wait_ge(s["c_tanh"], 2)
                        sc.activation(wv_split[:, 0], wv_sb[:], ACT.Copy).then_inc(s["wv_hi"], 1)
                        sc.activation(extra[:, :, E:E + 1], tg[0:S, 1:2].unsqueeze(1).to_broadcast([S, G, 1]), ACT.Copy).then_inc(s["c_tanh"], 1)
                    if k < 2 and group_there(j, -2):
                        hot_rows(n, 2 * k)
                    if there(j, k, 0):
                        n.wait(s["av_ps"], 4, k + 1)
                        sc.activation(avT[:, 0], ps_v[:, 0:2 * S].rearrange("p (k q) -> p k q", k=2), ACT.Copy).then_inc(s["av_hi"], 1)
                    if k < 2 and group_there(j, -2):
                        hot_rows(n, 2 * k + 1)
                    if there(j, k, 1):
                        proj(n, k, 1)
                    if there(j, k, 2):
                        head(n, k, 2)
                    if isinstance(j, int) and j == 1:
                        split_gate_up(0, lambda m: m, [k])
                    if isinstance(j, int) and (j, k) == (1, 3):
                        split_down(0, lambda m: m)

            n = Counts(act_e, 0)
            head(n, -2, 2)
            act_e.wait_ge(s["proj_in"], 64)
            proj(n, -1, 1)
            head(n, -1, 2)
            groups(act_e, steps)

            act_e.wait_ge(s["plan_ok"], 1)

            def next_hT(u1):
                act_e.wait_ge(s["gT_ps"], u1)
                sc.activation(hgT[:, 0, :], bank[0][:], ACT.Copy).then_inc(s["gT_hi"], 1)

            def unit(g, ft):
                g1 = act_e.snap(g + 1)

                def upper(f):
                    act_e.wait_ge(prod_ok[f], g1)
                    sc.activation(act[:, 0, f, :], prod[:, f, :], ACT.Copy).then_inc(hi_ok[f], 1)

                for f in range(ft):
                    act_e.wait_ge(gu_ps[f], g1)
                    sc.activation(gel[:, f, :], bank[1 + f][:, 0:UNIT], ACT.Gelu).then_inc(gel_ok[f], 1)
                    if f > 0:
                        upper(f - 1)
                upper(ft - 1)
                next_hT(act_e.snap(g + 2))

            next_hT(1)
            with act_e.Fori(0, E // 2) as i2:
                for q in range(2):
                    if q == 0:
                        lo = act_e.value_load(cum_i[0:1, bass.ds(i2 * 2, 1)], min_val=0, max_val=UNITS - 3)
                    hi = act_e.value_load(cum_i[0:1, bass.ds(i2 * 2 + (q + 1), 1)], min_val=1, max_val=UNITS - 3)
                    count = lambda m: act_e.snap(i2 * (2 * m) + (q + 2) * m)
                    if q == 0:
                        sc.activation(gate_copy[:], gates[:], ACT.Gelu)
                    act_e.wait_ge(s["dn_ps"], act_e.snap(lo + 1))
                    split_gate_up(1 - q, count)
                    with act_e.Fori(lo, hi) as g:
                        unit(g, 4)
                    split_down(1 - q, count)
                    lo = hi
            lo = act_e.value_load(cum_i[0:1, E:E + 1], min_val=E, max_val=UNITS - 3)
            hi = act_e.value_load(cum_i[0:1, E + 1:E + 2], min_val=E + 1, max_val=UNITS - 3)
            with act_e.Fori(lo, hi) as g:
                unit(g, 1)

        @block.vector
        def _(dve):
            own = Chain(dve, s["dve_own"])
            v = nc.vector
            dve.sem_inc(s["yo_ok"], 2)
            dve.wait_ge(s["c_gp"], 1)
            own.put(v.tensor_copy(before_r[:], before[:]))
            own.put(v.tensor_copy(ones_r[:], ones[0:S, :]))
            own.put(v.tensor_copy(ids[:, 0, :], ids_i[:]))
            own.put(v.tensor_scalar(ids[:, 1, :], ids_i[:], -1.0, None, ALU.mult))
            own.put(v.tensor_copy(dummy_f[:], dummy_i[:]))
            own.link(v.tensor_copy(iota_f[:], iota_i[:]))
            own.put(v.tensor_scalar(rev8[:], iota_f[0:S, 0:E], -1.0, float(E), ALU.mult, ALU.add))
            own.wait()
            dve.sem_inc(s["c_dve"], 1)

            def stats1(n, k, off):
                slot, p = (k + off) % 4, (k + off) % 2
                n.wait(x_in[slot], 16, 16 * ((k + off) // 4 + 1))
                own.link(v.bn_stats(stat1[:, p, :], x_sb[:, slot, :]))
                v.bn_aggr(mv1[:, p, :], stat1[:, p, :]).then_inc(s["st1"], 1)

            def normal1(n, k, off):
                slot, p = (k + off) % 4, (k + off) % 2
                n.wait(s["rs1_ok"], 4, k + off + 1)
                n.wait(s["yT_ps"], 4, k + off - 1)
                v.tensor_scalar(y_sb[:, p, :], x_sb[:, slot, :], mv1[:, p, 0:1], rs1[:, p, :],
                                ALU.subtract, ALU.mult).then_inc(s["y_ok"], 1)

            def top2():
                rev = rev8[:].unsqueeze(1).to_broadcast([S, G, E])
                own.link(v.tensor_reduce(out=m12[:, 0, :], in_=logit[:], axis=AX.X, op=ALU.max))
                src = logit
                for i in range(2):
                    mx = m12[:, i, :].unsqueeze(2).to_broadcast([S, G, E])
                    own.link(v.tensor_tensor(eq[:], src[:], mx, ALU.is_equal))
                    own.link(v.tensor_tensor(eq[:], eq[:], rev, ALU.mult))
                    own.link(v.tensor_reduce(out=mi3[:, :, i], in_=eq[:], axis=AX.X, op=ALU.max))
                    own.link(v.tensor_tensor(oh[:, :, i, :], rev, mi3[:, :, i:i + 1].to_broadcast([S, G, E]), ALU.is_equal))
                    if i == 0:
                        own.link(v.scalar_tensor_tensor(rest[:], oh[:, :, 0, :], -1e30, logit[:], ALU.mult, ALU.add))
                        own.link(v.tensor_reduce(out=m12[:, 1, :], in_=rest[:], axis=AX.X, op=ALU.max))
                        src = rest
                own.link(v.tensor_tensor(rest[:], logit[:], m12[:, 0, :].unsqueeze(2).to_broadcast([S, G, E]), ALU.subtract))
                own.put(v.tensor_tensor(expo[:].rearrange("p (g e) -> p g e", e=E), rest[:],
                                        inv_g[:].unsqueeze(2).to_broadcast([S, G, E]), ALU.mult))
                own.link(v.tensor_copy(extra[:, :, E + 1], inv_g[:]))
                v.tensor_tensor(cnt[:], oh[:, :, 0, :], oh[:, :, 1, :], ALU.add).then_inc(s["top_ok"], 1)

            def carry_on(total, counts, n_e):
                own.link(v.tensor_reduce(out=csum[:, 0:n_e], in_=counts[:].bitcast(F32).rearrange("p g e -> p e g"), axis=AX.X, op=ALU.add))
                own.link(v.tensor_tensor(total[:, 0:n_e], total[:, 0:n_e].bitcast(F32), csum[:, 0:n_e], ALU.add))

            def one_pos(n, src, psem, rsem, dst):
                n.wait(s[psem], 1, 0)
                v.tensor_tensor(pm[:], oh[:], src.unsqueeze(2).to_broadcast([S, G, 2, E]), ALU.mult).then_inc(s[rsem], 1)
                n.wait(s[rsem], 1, 0)
                own.link(v.tensor_reduce(out=dst, in_=pm[:], axis=AX.X, op=ALU.add))

            def overflow(n):
                own.link(v.tensor_scalar(drop[:], pos[:], float(CAP), None, ALU.is_ge))
                own.link(v.tensor_reduce(out=ovf[:], in_=drop[:], axis=AX.X, op=ALU.max))
                own.link(v.tensor_scalar(keep[:], ovf[:], -1.0, 1.0, ALU.mult, ALU.add))
                own.put(v.tensor_copy(cnt2[:, :, E:E + 1], ovf[:].unsqueeze(2)))
                v.tensor_tensor(cnt2[:, :, 0:E], cnt[:].bitcast(F32), keep[:].unsqueeze(2).to_broadcast([S, G, E]),
                                ALU.mult).then_inc(s["cnt2_ok"], 1)
                own.wait()
                n.wait(s["cnt2_ok"], 1, 0)

            def slots(n):
                own.put(v.tensor_scalar(pen[:, :, 0:2], ovf[:].unsqueeze(2).to_broadcast([S, G, 2]), 16384.0, float(E * CAP), ALU.mult, ALU.add))
                own.put(v.tensor_scalar(pen[:, :, 2:3], keep[:].unsqueeze(2), 16384.0, float(E * CAP), ALU.mult, ALU.add))
                own.link(v.scalar_tensor_tensor(cpos[:], mi3[:], -float(CAP), cpos[:], ALU.mult, ALU.add))
                own.link(v.tensor_tensor(slot_i[:].rearrange("p (g c) -> p g c", c=3), cpos[:], pen[:], ALU.add))
                own.put(v.tensor_single_scalar(lc_i[:, 0, :], slot_i[:], 127, ALU.bitwise_and))
                own.link(v.tensor_single_scalar(lc_i[:, 1, :], slot_i[:], 7, ALU.logical_shift_right))
                for i, sign in enumerate((1, -1)):
                    own.put(v.tensor_scalar(ids[:, i, :], ids[:, i, :], float(sign * G * S), None, ALU.add))
                own.wait()
                v.tensor_copy(lc[:], lc_i[:]).then_inc(s["lc_ok"], 1)

            def softmax(n):
                n.wait(s["ex_ok"], 1, 0)
                own.link(v.reciprocal(ex[:], sg[:, 1, :]))
                own.link(v.tensor_tensor(ex[:], ex[:], sg[:, 0, :], ALU.mult))
                own.link(v.tensor_reduce(out=den[:, 0, :], in_=ex[:].rearrange("p (g e) -> p g e", e=E), axis=AX.X, op=ALU.add))
                own.link(v.reciprocal(den[:, 1, :], den[:, 0, :]))
                own.put(v.tensor_scalar(den[:, 0, :], den[:, 1, :], tg[0:S, 1:2], None, ALU.mult))

            def weights(n):
                own.link(v.tensor_tensor(wnum[:], ex[:].rearrange("p (g e) -> p g e", e=E), cnt2[:, :, 0:E].bitcast(F32), ALU.mult))
                v.tensor_tensor(extra[:, :, 0:E], wnum[:], den[:, 0, :].unsqueeze(2).to_broadcast([S, G, E]),
                                ALU.mult).then_inc(s["wd_ok"], 1)

            def hot_cols(n):
                v.tensor_tensor(hot_col[:], iota_f[0:S, 0:TABLE].unsqueeze(1).to_broadcast([S, 3 * G, TABLE]),
                                lc[:, 1, :].unsqueeze(2).to_broadcast([S, 3 * G, TABLE]), ALU.is_equal).then_inc(s["hot_ok"], 1)

            def add_table(n):
                n.wait(s["tab_ps"], 1, -1)
                v.tensor_tensor(table[:], table[:], r_tab, ALU.add).then_inc(s["tab_ok"], 1)

            def split_gate_up(q, count, parts=range(4)):
                for i in parts:
                    k, w, raw = ((0, wg_sb[q], raw_g), (0, wu_sb[q], raw_u), (1, wg_sb[q], raw_g), (1, wu_sb[q], raw_u))[i]
                    dve.wait_ge(s["gu_hi"], count(4, i - 3))
                    v.scalar_tensor_tensor(w[:, 1, k, :], raw[:, k, :], raw_n[:, k:k + 1],
                                           w[:, 0, k, :].bitcast(F32), ALU.mult, ALU.subtract).then_inc(s["gu_split"], 1)

            def split_down(q, count):
                dve.wait_ge(s["wd_hi"], count(1, 0))
                v.tensor_tensor(wd_sb[q][:, 1], raw_d[:], wd_sb[q][:, 0].bitcast(F32), ALU.subtract).then_inc(s["wd_split"], 1)

            def steps(j):
                n = Counts(dve, j)
                tail = isinstance(j, int) and j > LAST
                for k in range(4):
                    if there(j, k, 2):
                        stats1(n, k, 2)
                    if there(j, k, -1):
                        p, slot = (k - 1) % 2, (k - 1) % 4
                        n.wait(s["o_ps"], 4, k)
                        n.wait(s["base_ok"], 4, k - 2)
                        v.tensor_tensor(x1[:, p, :], ps_o[0:S, 0:H], x_sb[:, slot, :], ALU.add).then_inc(s["x1_ok"], 1)
                        n.wait(s["x1_ok"], 4, k)
                        own.link(v.bn_stats(stat2[:, p, :], x1[:, p, :]))
                        v.bn_aggr(mv2[:, p, :], stat2[:, p, :]).then_inc(s["st2"], 1)
                        if k == 0 and tail:
                            n.wait(s["lc_ok"], 1, -1)
                            hot_cols(n)
                    if k == 2 and group_there(j, -1):
                        if tail:
                            softmax(n)
                        one_pos(n, r_pos, "pos_ps", "pos_rd", pos[:])
                        overflow(n)
                    if k == 3 and group_there(j, -1):
                        n.wait(s["pos2_ps"], 1, 0)
                        own.put(v.tensor_copy(cpos[:, :, 2:3], r_pos2[:, :, E:E + 1]))
                        one_pos(n, r_pos2[:, :, 0:E], "pos2_ps", "pos2_rd", cpos[:, :, 0:2])
                    if isinstance(j, int) and (j, k) == (0, 0):
                        dve.wait_ge(s["wv_hi"], 1)
                        v.tensor_tensor(wv_split[:, 1], wv_sb[:], wv_split[:, 0].bitcast(F32), ALU.subtract).then_inc(s["wv_ok"], 1)
                    if there(j, k, 0):
                        n.wait(s["av_hi"], 4, k + 1)
                        v.tensor_tensor(avT[:, 1], ps_v[:, 0:2 * S].rearrange("p (k q) -> p k q", k=2), avT[:, 0].bitcast(F32),
                                        ALU.subtract).then_inc(s["av_ok"], 1)
                    if there(j, k, 2):
                        normal1(n, k, 2)
                    if there(j, k, -1):
                        n.wait(s["rs3_ok"], 4, k)
                        n.wait(h_out[p], 32, 16 * ((k - 1) // 2))
                        v.tensor_scalar(h_sb[:, p, :], x1[:, p, :], mv2[:, p, 0:1], rs3[:, p, 0:1],
                                        ALU.subtract, ALU.mult).then_inc(s["h_ok"], 1)
                    if k == 2 and group_there(j, -1):
                        carry_on(carry, cnt, E)
                        if not tail:
                            softmax(n)
                    if k == 3 and group_there(j, -1):
                        slots(n)
                        carry_on(carry2, cnt2, E2)
                        if tail:
                            dve.sem_inc(s["carried"], 1)
                            dve.wait_ge(s["lc_ok"], B // G)
                            hot_cols(n)
                        weights(n)
                    if k == 0 and group_there(j, -2) and not tail:
                        n.wait(s["lc_ok"], 1, -1)
                        hot_cols(n)
                    if there(j, k, -2):
                        p = k % 2
                        n.wait(s["inv_ok"], 4, k - 1)
                        v.tensor_copy(inv_g[:, (k - 2) % 4:(k - 2) % 4 + 1], inv_t[:, p, :]).then_inc(s["inv_rd"], 1)
                        n.wait(s["lg_ps"], 4, k - 1)
                        v.tensor_copy(logit[:, (k - 2) % 4, :], r_logit).then_inc(s["lg_ok"], 1)
                    if k == 1 and group_there(j, -1):
                        n.wait(s["lg_ok"], 4, k - 1)
                        n.wait(s["inv_rd"], 4, k - 1)
                        if isinstance(j, int) and j == 1:
                            dve.wait_ge(s["c_tanh"], 4)
                        n.wait(s["ext_out"], 16, -16)
                        top2()
                    if k == 1 and group_there(j, -2):
                        add_table(n)
                    if isinstance(j, int) and j == 1:
                        split_gate_up(0, lambda m, c: m + c, [k])
                    if isinstance(j, int) and (j, k) == (1, 3):
                        split_down(0, lambda m, c: m + c)
                own.restart()

            n = Counts(dve, 0)
            stats1(n, -2, 2)
            normal1(n, -2, 2)
            stats1(n, -1, 2)
            normal1(n, -1, 2)
            own.restart()
            groups(dve, steps, last=LAST + 2)

            dve.wait_ge(s["tot_ps"], 1)
            own.link(v.tensor_scalar(tot_i[:], r_tot[:, 0:E + 1], float(UNIT - 1), None, ALU.add))
            own.link(v.tensor_single_scalar(tot_i[:], tot_i[:], 8, ALU.logical_shift_right))
            own.link(v.tensor_scalar(nun[:], tot_i[:], 1.0, None, ALU.max))
            own.put(v.memset(cum[:, :, 0:1], 0.0))
            own.link(v.tensor_copy(cum[:, 0, 1:E + 2], nun[:]))
            step, at = 1, 0
            while step < E + 1:
                own.put(v.tensor_copy(cum[:, 1 - at, 1:step + 1], cum[:, at, 1:step + 1]))
                own.link(v.tensor_tensor(cum[:, 1 - at, step + 1:E + 2], cum[:, at, step + 1:E + 2], cum[:, at, 1:E + 2 - step], ALU.add))
                step, at = 2 * step, 1 - at
            own.put(v.tensor_copy(cum_i[:], cum[:, at, :]))
            own.put(v.tensor_scalar(step8[:], nun[:, 0:E], -2.0, float(CAP // 128), ALU.mult, ALU.add))
            own.link(v.tensor_tensor(begun[:], iota_f[:, 0:UNITS].unsqueeze(2).to_broadcast([128, UNITS, E + 1]),
                                     cum[:, at, 1:E + 2].unsqueeze(1).to_broadcast([128, UNITS, E + 1]), ALU.is_ge))
            own.link(v.tensor_tensor(ucol3[:], begun[:, :, 0:E], step8[:].unsqueeze(1).to_broadcast([128, UNITS, E]), ALU.mult))
            own.link(v.tensor_reduce(out=ucol_f[:], in_=ucol3[:], axis=AX.X, op=ALU.add))
            own.link(v.scalar_tensor_tensor(ucol[:], iota_f[:, 0:UNITS], 2.0, ucol_f[:], ALU.mult, ALU.add))
            dve.sem_inc(s["plan_ok"], 1)
            add_table(Counts(dve, LAST + 2))
            dve.wait_ge(s["tab_ok"], B // G)
            own.put(v.tensor_scalar(gidx[:], table[:], 1.0, -1.0, ALU.max, ALU.add))
            own.link(v.tensor_scalar(empty[:], table[:], 0.0, None, ALU.is_equal))
            own.link(v.tensor_tensor(empty[:].rearrange("p (u c) -> p u c", c=2), empty[:].rearrange("p (u c) -> p u c", c=2),
                                     dummy_f[:].unsqueeze(1).to_broadcast([128, TABLE // 2, 2]), ALU.mult))
            own.put(v.scalar_tensor_tensor(sidx[:], table[:], -1.0, empty[:], ALU.add, ALU.add))
            own.wait()
            dve.sem_inc(s["rows_ok"], 1)
            own.put(v.tensor_scalar(uhot[:, :, 0:1], begun[:, :, 0:1], -1.0, 1.0, ALU.mult, ALU.add))
            own.link(v.tensor_tensor(uhot[:, :, 1:E + 1], begun[:, :, 0:E], begun[:, :, 1:E + 1], ALU.subtract))
            own.restart()

            def weights_of(u, u16):
                for i in range(2):
                    dve.wait_ge(hg_in[i], u16)
                own.link(v.tensor_tensor(w9[:], hg[:, :, H:W_FB + 1], uhot[:, bass.ds(u, 1), :].to_broadcast([128, 2, E + 1]), ALU.mult))
                own.put(v.tensor_reduce(out=w_next[:], in_=w9[:], axis=AX.X, op=ALU.add))
                own.link(v.tensor_reduce(out=w_exp[:], in_=w9[:, :, 0:E], axis=AX.X, op=ALU.add))
                v.tensor_tensor(wi_next[:], w_exp[:], hg[:, :, W_INV], ALU.mult).then_inc(s["wi_ok"], 1)

            def next_hT(u1):
                dve.wait_ge(s["gT_hi"], u1)
                v.tensor_tensor(hgT[:, 1, :], bank[0][:], hgT[:, 0, :].bitcast(F32), ALU.subtract).then_inc(s["gT_ok"], 1)

            def unit(g, ft):
                g1 = dve.snap(g + 1)
                g2 = dve.snap(g + 2)

                def product(f):
                    dve.wait_ge(gel_ok[f], g1)
                    v.tensor_tensor(prod[:, f, :], gel[:, f, :], bank[1 + f][:, UNIT:2 * UNIT], ALU.mult).then_inc(prod_ok[f], 1)

                def lower(f):
                    dve.wait_ge(hi_ok[f], g1)
                    v.tensor_tensor(act[:, 1, f, :], prod[:, f, :], act[:, 0, f, :].bitcast(F32), ALU.subtract).then_inc(act_ok[f], 1)

                for f in range(ft):
                    product(f)
                    if f > 0:
                        lower(f - 1)
                    if f == min(2, ft - 1):
                        weights_of(g + 1, dve.snap(g * 16 + 32))
                lower(ft - 1)
                next_hT(g2)
                dve.wait_ge(s["yo_free"], g1)
                dve.wait_ge(s["hw_ok"], g1)
                dve.wait_ge(s["dn_ps"], g2)
                par = dve.snap(g & 1)
                for i in range(2):
                    ins = v.scalar_tensor_tensor(yo[:, i, :], bank[5 + i][:, 0:H], w_now[:, i:i + 1],
                                                 hw[:, bass.ds(par * 2 + i, 1), :].rearrange("p o d -> p (o d)"), ALU.mult, ALU.add)
                    ins.then_inc(s["yo_ok"], 1)
                dve.wait_ge(s["yo_ok"], dve.snap(g * 2 + 4))
                own.put(v.tensor_copy(w_now[:], w_next[:]))
                own.restart()

            weights_of(0, 16)
            own.link(v.tensor_copy(w_now[:], w_next[:]))
            own.restart()
            next_hT(1)
            with dve.Fori(0, E // 2) as i2:
                for q in range(2):
                    if q == 0:
                        lo = dve.value_load(cum_i[0:1, bass.ds(i2 * 2, 1)], min_val=0, max_val=UNITS - 3)
                    hi = dve.value_load(cum_i[0:1, bass.ds(i2 * 2 + (q + 1), 1)], min_val=1, max_val=UNITS - 3)
                    count = lambda m, c: dve.snap(i2 * (2 * m) + ((q + 2) * m + c))
                    split_gate_up(1 - q, count)
                    own.restart()
                    with dve.Fori(lo, hi) as g:
                        unit(g, 4)
                    split_down(1 - q, count)
                    lo = hi
            lo = dve.value_load(cum_i[0:1, E:E + 1], min_val=E, max_val=UNITS - 3)
            hi = dve.value_load(cum_i[0:1, E + 1:E + 2], min_val=E + 1, max_val=UNITS - 3)
            with dve.Fori(lo, hi) as g:
                unit(g, 1)

        @block.tensor
        def _(pe):
            t = nc.tensor

            def mm(o, l, r, first, last):
                return t.matmul(o, l, r, start=first, stop=last)

            def transposes(n, k, off):
                slot, p, c = (k + off) % 4, (k + off) % 2, k + off + 1
                n.wait(ctx_in[slot], 32, 32 * ((k + off) // 4 + 1))
                for h, bk_ in enumerate((ps_c0, ps_c1)):
                    n.wait(s[f"c{h}_ok"], 4, c - 1)
                    for i in range(3):
                        last = t.transpose(bk_[:, i * KC:(i + 1) * KC], ctx_sb[:, slot, i, h * 128:(h + 1) * 128], ident[0:KC, 0:KC])
                    last.then_inc(s[f"c{h}_ps"], 1)
                n.wait(s["y_ok"], 4, c)
                n.wait(s["qp_ok"], 4, c - 1)
                for h in range(2):
                    last = t.transpose(ps_q[:, h * S:(h + 1) * S], y_sb[:, p, h * 128:(h + 1) * 128], ident[0:S, 0:S])
                last.then_inc(s["yT_ps"], 1)

            def projections(n, k, off):
                c = k + off + 1
                n.wait(s["c0_ok"], 4, c)
                n.wait(s["c1_ok"], 4, c)
                n.wait(s["kp_ok"], 4, c - 1)
                for h in range(2):
                    last = mm(ps_k[0:QK, 0:C], wk_sb[:, h, :], ctxT[:, h, :], h == 0, h == 1)
                last.then_inc(s["kp_ps"], 1)
                n.wait(s["yT_ok"], 4, c)
                for h in range(2):
                    last = mm(ps_q[0:QK, 2 * S:3 * S], wq_sb[:, h, :], yT[:, h, :], h == 0, h == 1)
                last.then_inc(s["qp_ps"], 1)

            def ranks(n, dst, counts, total, n_e, ok, ps):
                n.wait(s[ok], 1, 0)
                mm(dst, before_r[:], counts[:], True, False)
                for i in range(G - 1):
                    mm(dst[:, i + 1:G, :], ones_r[:, 0:S], counts[:, i, :].unsqueeze(1).to_broadcast([S, G - 1 - i, n_e]), False, False)
                mm(dst, ones_r[:, 0:S], total[:, 0:n_e].unsqueeze(1).to_broadcast([S, G, n_e]), False, True).then_inc(s[ps], 1)

            def table_part(n):
                n.wait(s["hot_ok"], 1, -1)
                for i in range(3 * G):
                    if i % 3 == 0:
                        n.wait(s["hlo_ok"], 4, i // 3 - 7)
                    last = mm(r_tab, hot_lo[:, i, :], hot_col[:, i, :], i == 0, i == 3 * G - 1)
                last.then_inc(s["tab_ps"], 1)

            def steps(j):
                n = Counts(pe, j)
                tail = isinstance(j, int) and j == LAST + 1
                for k in range(4):
                    if there(j, k, 0):
                        n.wait(s["kp_ok"], 4, k + 1)
                        n.wait(s["qp_ok"], 4, k + 1)
                        n.wait(s["z_ok"], 4, k)
                        for i in range(3):
                            last = mm(ps_s[0:KC, i * S:(i + 1) * S], kpT[:, i * KC:(i + 1) * KC], qpT[:], True, True)
                        last.then_inc(s["s_ps"], 1)
                    if there(j, k, -2):
                        p = k % 2
                        n.wait(s["h_ok"], 4, k - 1)
                        n.wait(s["av_ok"], 4, k if there(j, k, -1) else k - 1)
                        for h in range(2):
                            last = t.transpose(ps_v[:, (2 + h) * S:(3 + h) * S], h_sb[:, p, h * 128:(h + 1) * 128], ident[0:S, 0:S])
                        last.then_inc(s["hT_ps"], 1)
                    if there(j, k, -1):
                        p = (k - 1) % 2
                        n.wait(s["av_ok"], 4, k)
                        n.wait(s["x1_ok"], 4, k - 1)
                        if isinstance(j, int) and (j, k) == (0, 1):
                            pe.wait_ge(s["c_tanh"], 3)
                            pe.wait_ge(s["wv_ok"], 1)
                        for h in range(2):
                            for a, b in PARTS:
                                mm(ps_o[0:S, 0:H], avT[:, a, h, :], wv_split[:, b, h, :], h == 0 and (a, b) == (0, 0), False)
                        n.wait(s["zs_ok"], 4, k)
                        mm(ps_o[0:S, 0:H], zs[:], bv_sb[:], False, True).then_inc(s["o_ps"], 1)
                    if there(j, k, 0):
                        slot = k % 4
                        n.wait(s["z_ok"], 4, k + 1)
                        n.wait(s["hT_ok"], 4, k - 1)
                        for h in range(2):
                            for i in range(3):
                                last = mm(ps_v[:, h * S:(h + 1) * S], ctx_sb[:, slot, i, h * 128:(h + 1) * 128],
                                          z_sb[:, k % 2, i, :], i == 0, i == 2)
                        last.then_inc(s["av_ps"], 1)
                    if k > 1 and group_there(j, -1):
                        n.wait(s["lg_ok"], 4, min(k - 2, B - 4 * j) if isinstance(j, int) else k - 2)
                    if k == 2 and group_there(j, -1):
                        if group_there(j, -2):
                            n.wait(s["tab_ok"], 1, -1)
                        ranks(n, r_pos, cnt, carry, E, "top_ok", "pos_ps")
                    if k == 3 and group_there(j, -1):
                        ranks(n, r_pos2, cnt2, carry2, E2, "cnt2_ok", "pos2_ps")
                        if tail:
                            pe.wait_ge(s["carried"], 1)
                            mm(r_tot[:, 0:E + 1], ones[0:S, :], carry2[:, 0:E + 1].bitcast(F32), True, True).then_inc(s["tot_ps"], 1)
                    if there(j, k, 1):
                        projections(n, k, 1)
                    if there(j, k, -2):
                        n.wait(s["hT_ok"], 4, k - 1)
                        n.wait(s["lg_ok"], 4, k - 2)
                        if k == 2 and group_there(j, -1):
                            n.wait(s["pos_rd"], 1, 0)
                        if k == 3 and group_there(j, -1):
                            n.wait(s["pos2_rd"], 1, 0)
                        for h in range(2):
                            last = mm(r_logit, hT[:, h, :], wr_sb[:, h, :], h == 0, h == 1)
                        last.then_inc(s["lg_ps"], 1)
                    if there(j, k, 2):
                        transposes(n, k, 2)
                    if k == 1 and group_there(j, -2):
                        n.wait(s["lg_ok"], 4, min(0, B - 4 * j) if isinstance(j, int) else 0)
                        table_part(n)

            pe.wait_ge(s["c_gp"], 1)
            n = Counts(pe, 0)
            transposes(n, -2, 2)
            pe.wait_ge(s["proj_in"], 64)
            projections(n, -1, 1)
            transposes(n, -1, 2)
            pe.wait_ge(s["c_dve"], 1)
            groups(pe, steps)
            pe.wait_ge(s["plan_ok"], 1)

            def next_hT(u16):
                for i in range(2):
                    pe.wait_ge(hg_in[i], u16)
                    for h in range(2):
                        last = t.transpose(bank[0][:, h * UNIT + i * 128:h * UNIT + (i + 1) * 128],
                                           hg[:, i, h * 128:(h + 1) * 128], ident[:])
                last.then_inc(s["gT_ps"], 1)

            def unit(g, e1, ft, q):
                g1 = pe.snap(g + 1)
                pe.wait_ge(s["gT_ok"], g1)
                for f in range(ft):
                    for i, w in enumerate((wg_sb[q], wu_sb[q])):
                        for h in range(2):
                            for a, b in PARTS:
                                last = mm(bank[1 + f][:, i * UNIT:(i + 1) * UNIT], w[:, a, h, f * 128:(f + 1) * 128],
                                          hgT[:, b, h * UNIT:(h + 1) * UNIT],
                                          h == 0 and (a, b) == (0, 0), h == 1 and (a, b) == (1, 0))
                    last.then_inc(gu_ps[f], 1)
                next_hT(pe.snap(g * 16 + 32))
                pe.wait_ge(s["yo_ok"], pe.snap(g * 2 + 2))
                pe.wait_ge(s["wd_split"], e1)
                for f in range(ft):
                    pe.wait_ge(act_ok[f], g1)
                    for i in range(2):
                        for a, b in PARTS:
                            last = mm(bank[5 + i][:, 0:H], act[:, a, f, i * 128:(i + 1) * 128], wd_sb[q][:, b, f, :],
                                      f == 0 and (a, b) == (0, 0), f == ft - 1 and (a, b) == (1, 0))
                    if f == ft - 1:
                        last.then_inc(s["dn_ps"], 1)

            next_hT(16)
            with pe.Fori(0, E // 2) as i2:
                for q in range(2):
                    if q == 0:
                        lo = pe.value_load(cum_i[0:1, bass.ds(i2 * 2, 1)], min_val=0, max_val=UNITS - 3)
                    hi = pe.value_load(cum_i[0:1, bass.ds(i2 * 2 + (q + 1), 1)], min_val=1, max_val=UNITS - 3)
                    e1 = pe.snap(i2 * 2 + (q + 1))
                    pe.wait_ge(s["gu_split"], pe.snap(i2 * 8 + 4 * (q + 1)))
                    settle(pe, s["settled"])
                    with pe.Fori(lo, hi) as g:
                        unit(g, e1, 4, q)
                    lo = hi
            lo = pe.value_load(cum_i[0:1, E:E + 1], min_val=E, max_val=UNITS - 3)
            hi = pe.value_load(cum_i[0:1, E + 1:E + 2], min_val=E + 1, max_val=UNITS - 3)
            pe.wait_ge(s["gu_split"], 4 * (E + 1))
            settle(pe, s["settled"])
            with pe.Fori(lo, hi) as g:
                unit(g, E + 1, 1, 0)


def kernel(**inputs):
    import numpy as _np
    import concourse.bacc as _bacc
    from concourse.bass_utils import run_bass_kernel_spmd as _run

    a = {k: _np.asarray(v) for k, v in inputs.items()}
    norms = _np.concatenate([a["L0_ffn_norm_w"], a["L0_ffn_f_norm"][None]], 0)
    arrays = {
        "x": a["x"].reshape(N, H),
        "ctx_rows": a["ctx_1024"].reshape(B * C, H),
        "g2": _np.concatenate([a["g_xattn"], a["g_ffn"]]),
        "wqT": a["L0_xattn_Wq"].T, "bq": a["L0_xattn_bq"],
        "wkT": a["L0_xattn_Wk"].T, "bk": a["L0_xattn_bk"],
        "wvT": a["L0_xattn_Wv"].T, "bv": a["L0_xattn_bv"],
        "wr": a["L0_ffn_Wr"],
        "norms": norms.reshape(E + 1, 2, 128).transpose(2, 0, 1),
        "wg": a["L0_ffn_Wg"], "wu": a["L0_ffn_Wu"], "wd": a["L0_ffn_Wd"],
        "fwg": a["L0_ffn_fWg"], "fwu": a["L0_ffn_fWu"], "fwd": a["L0_ffn_fWd"],
    }
    arrays = {k: _np.ascontiguousarray(v) for k, v in arrays.items()}
    nc = _bacc.Bacc("TRN2", target_bir_lowering=False, num_devices=1)
    args = [nc.dram_tensor(k, v.shape, mybir.dt.from_np(v.dtype), kind="ExternalInput").ap() for k, v in arrays.items()]
    out = nc.dram_tensor("out", [N + DUMMY, H], F32, kind="ExternalOutput").ap()
    build(nc, *args, out)
    r = _run(nc, [arrays], core_ids=[0])
    return r.results[0]["out"][:N].reshape(B, S, H)
```
